# Optimizing a Trainium2 kernel written in Bass

```python
import numpy as np
import jax
import jax.numpy as jnp

def _softmax(x, axis=-1):
    return jax.nn.softmax(x, axis=axis)

def _gelu(x):
    return jax.nn.gelu(x, approximate=True)

def _silu(x):
    return jax.nn.silu(x)

def _sigmoid(x):
    return jax.nn.sigmoid(x)

def _layernorm(x, axis=-1, eps=1e-05):
    m = jnp.mean(x, axis=axis, keepdims=True)
    v = jnp.var(x, axis=axis, keepdims=True)
    return (x - m) / jnp.sqrt(v + eps)

def _scatter_add(tgt, idx, src, axis=0):
    return tgt.at[idx].add(src)

def _segment_sum(src, seg, n):
    return jax.ops.segment_sum(src, seg, n)
kernel_name = 'mk_macaron_d1_jaxref_r8_6b4119'

def setup_inputs(seed: int=0):
    np.random.seed(seed)
    _w = jnp.asarray

    def _L0_attn_setup():
        import jax, jax.numpy as jnp
        import numpy as np
        EMBED = 128
        HEADS = 16
        key = jax.random.key(seed)
        ks = jax.random.split(key, 6)
        N, S = (1, 512)
        half = EMBED // 2
        x = jax.random.normal(ks[0], (N, S, EMBED), dtype=jnp.float32)
        Wq = jax.random.normal(ks[1], (half, half), dtype=jnp.float32) * 0.02
        Wk = jax.random.normal(ks[2], (half, half), dtype=jnp.float32) * 0.02
        Wv = jax.random.normal(ks[3], (half, half), dtype=jnp.float32) * 0.02
        Wo = jax.random.normal(ks[4], (EMBED, half), dtype=jnp.float32) * 0.02
        bo = jnp.zeros((EMBED,), dtype=jnp.float32)
        return {'x': x, 'Wq': Wq, 'Wk': Wk, 'Wv': Wv, 'Wo': Wo, 'bo': bo}
    _L0_attn_in = _L0_attn_setup()

    def _L0_ffn_setup():
        import jax, jax.numpy as jnp
        import numpy as np
        D = 128
        H = 16
        DH = D // H
        DC = D // 4
        HID = 256
        G = 2
        EPG = 4
        E = G * EPG
        TOPK = 2
        EPS = 1e-06
        B, T = (2, 256)

        def _rope_sincos(t, dh):
            inv_freq = 1.0 / 10000.0 ** (jnp.arange(0, dh, 2, dtype=jnp.float32) / dh)
            ang = jnp.arange(t, dtype=jnp.float32)[:, None] * inv_freq[None, :]
            return (jnp.sin(ang), jnp.cos(ang))

        def _apply_rope(x, sin, cos):
            x1 = x[..., ::2]
            x2 = x[..., 1::2]
            r = jnp.stack([x1 * cos - x2 * sin, x1 * sin + x2 * cos], axis=-1)
            return r.reshape(x.shape)

        def _swiglu(x):
            a, b = jnp.split(x, 2, axis=-1)
            return jax.nn.silu(a) * b

        def _rmsnorm(x, w):
            return x * jax.lax.rsqrt(jnp.mean(x * x, axis=-1, keepdims=True) + EPS) * w
        key = jax.random.key(seed)
        ks = jax.random.split(key, 14)
        s = 0.02
        return {'src': jax.random.normal(ks[0], (B, T, D), jnp.float32), 'Wq': jax.random.normal(ks[1], (D, D), jnp.float32) * s, 'Wk_c': jax.random.normal(ks[2], (D, DC), jnp.float32) * s, 'Wv_c': jax.random.normal(ks[3], (D, DC), jnp.float32) * s, 'Wk': jax.random.normal(ks[4], (DC, D), jnp.float32) * s, 'Wv': jax.random.normal(ks[5], (DC, D), jnp.float32) * s, 'Wo': jax.random.normal(ks[6], (D, D), jnp.float32) * s, 'W_shared_in': jax.random.normal(ks[7], (D, 2 * HID), jnp.float32) * s, 'W_shared_out': jax.random.normal(ks[8], (HID, D), jnp.float32) * s, 'W1_shared': jax.random.normal(ks[9], (D, 2 * HID), jnp.float32) * s, 'W2_experts': jax.random.normal(ks[10], (E, HID, D), jnp.float32) * s, 'Wg_gate': jax.random.normal(ks[11], (D, G), jnp.float32) * s, 'We_gate': jax.random.normal(ks[12], (D, E), jnp.float32) * s, 'group_bias': jnp.zeros((G,), jnp.float32), 'expert_bias': jnp.zeros((E,), jnp.float32), 'norm1_w': jnp.ones((D,), jnp.float32), 'norm2_w': jnp.ones((D,), jnp.float32)}
    _L0_ffn_in = _L0_ffn_setup()
    _d = {'L0_attn_x': _L0_attn_in['x'], 'L0_attn_Wq': _L0_attn_in['Wq'], 'L0_attn_Wk': _L0_attn_in['Wk'], 'L0_attn_Wv': _L0_attn_in['Wv'], 'L0_attn_Wo': _L0_attn_in['Wo'], 'L0_attn_bo': _L0_attn_in['bo'], 'L0_ffn_Wq': _L0_ffn_in['Wq'], 'L0_ffn_Wk_c': _L0_ffn_in['Wk_c'], 'L0_ffn_Wv_c': _L0_ffn_in['Wv_c'], 'L0_ffn_Wk': _L0_ffn_in['Wk'], 'L0_ffn_Wv': _L0_ffn_in['Wv'], 'L0_ffn_Wo': _L0_ffn_in['Wo'], 'L0_ffn_W_shared_in': _L0_ffn_in['W_shared_in'], 'L0_ffn_W_shared_out': _L0_ffn_in['W_shared_out'], 'L0_ffn_W1_shared': _L0_ffn_in['W1_shared'], 'L0_ffn_W2_experts': _L0_ffn_in['W2_experts'], 'L0_ffn_Wg_gate': _L0_ffn_in['Wg_gate'], 'L0_ffn_We_gate': _L0_ffn_in['We_gate'], 'L0_ffn_group_bias': _L0_ffn_in['group_bias'], 'L0_ffn_expert_bias': _L0_ffn_in['expert_bias'], 'L0_ffn_norm1_w': _L0_ffn_in['norm1_w'], 'L0_ffn_norm2_w': _L0_ffn_in['norm2_w']}
    _x0 = _d['L0_attn_x']
    _d['L0_attn_x'] = jax.random.normal(jax.random.fold_in(jax.random.key(seed), 1), (4, 512, 128), dtype=_x0.dtype)
    del _x0
    return _d

def reference(L0_attn_x, L0_attn_Wq, L0_attn_Wk, L0_attn_Wv, L0_attn_Wo, L0_attn_bo, L0_ffn_Wq, L0_ffn_Wk_c, L0_ffn_Wv_c, L0_ffn_Wk, L0_ffn_Wv, L0_ffn_Wo, L0_ffn_W_shared_in, L0_ffn_W_shared_out, L0_ffn_W1_shared, L0_ffn_W2_experts, L0_ffn_Wg_gate, L0_ffn_We_gate, L0_ffn_group_bias, L0_ffn_expert_bias, L0_ffn_norm1_w, L0_ffn_norm2_w):

    def _L0_attn_ref(x, Wq, Wk, Wv, Wo, bo):
        import jax, jax.numpy as jnp
        import numpy as np
        EMBED = 128
        HEADS = 16
        N, S, E = x.shape
        H = HEADS
        Dh = E // 2 // H
        scale = float(E // H) ** 0.5
        left = x[..., :E // 2]
        q = (left @ Wq.T).reshape(N, S, H, Dh)
        k = (left @ Wk.T).reshape(N, S, H, Dh)
        v = (left @ Wv.T).reshape(N, S, H, Dh)
        energy = jnp.einsum('nqhd,nkhd->nqkh', q, k)
        att = jax.nn.softmax(energy / scale, axis=2)
        out = jnp.einsum('nqkh,nkhd->nqhd', att, v)
        out = out.reshape(N, S, E // 2)
        return out @ Wo.T + bo

    def _L0_ffn_ref(src, Wq, Wk_c, Wv_c, Wk, Wv, Wo, W_shared_in, W_shared_out, W1_shared, W2_experts, Wg_gate, We_gate, group_bias, expert_bias, norm1_w, norm2_w):
        import jax, jax.numpy as jnp
        import numpy as np
        D = 128
        H = 16
        DH = D // H
        DC = D // 4
        HID = 256
        G = 2
        EPG = 4
        E = G * EPG
        TOPK = 2
        EPS = 1e-06
        B, T = (2, 256)

        def _rope_sincos(t, dh):
            inv_freq = 1.0 / 10000.0 ** (jnp.arange(0, dh, 2, dtype=jnp.float32) / dh)
            ang = jnp.arange(t, dtype=jnp.float32)[:, None] * inv_freq[None, :]
            return (jnp.sin(ang), jnp.cos(ang))

        def _apply_rope(x, sin, cos):
            x1 = x[..., ::2]
            x2 = x[..., 1::2]
            r = jnp.stack([x1 * cos - x2 * sin, x1 * sin + x2 * cos], axis=-1)
            return r.reshape(x.shape)

        def _swiglu(x):
            a, b = jnp.split(x, 2, axis=-1)
            return jax.nn.silu(a) * b

        def _rmsnorm(x, w):
            return x * jax.lax.rsqrt(jnp.mean(x * x, axis=-1, keepdims=True) + EPS) * w
        Bb, Tt, C = src.shape
        q = (src @ Wq).reshape(Bb, Tt, H, DH).transpose(0, 2, 1, 3)
        k = (src @ Wk_c @ Wk).reshape(Bb, Tt, H, DH).transpose(0, 2, 1, 3)
        v = (src @ Wv_c @ Wv).reshape(Bb, Tt, H, DH).transpose(0, 2, 1, 3)
        sin, cos = _rope_sincos(Tt, DH)
        q = _apply_rope(q, sin, cos)
        k = _apply_rope(k, sin, cos)
        attn = jnp.einsum('bhqd,bhkd->bhqk', q, k) / np.sqrt(DH).astype(np.float32)
        attn = jax.nn.softmax(attn, axis=-1)
        sa = jnp.einsum('bhqk,bhkd->bhqd', attn, v)
        sa = sa.transpose(0, 2, 1, 3).reshape(Bb, Tt, C) @ Wo
        x = _rmsnorm(src + sa, norm1_w)
        S = Bb * Tt
        flat = x.reshape(S, C)
        shared = _swiglu(flat @ W_shared_in) @ W_shared_out
        g_probs = jax.nn.softmax(flat @ Wg_gate + group_bias, -1)
        g_idx = jnp.argmax(g_probs, axis=-1)
        e_logits = flat @ We_gate + expert_bias
        e_group = jnp.arange(E) // EPG
        in_group = e_group[None, :] == g_idx[:, None]
        e_probs = jax.nn.softmax(jnp.where(in_group, e_logits, -jnp.inf), -1)
        g_prob = jnp.take_along_axis(g_probs, g_idx[:, None], axis=1)
        p_expert = e_probs * g_prob
        topv, topi = jax.lax.top_k(p_expert, TOPK)
        w = jnp.zeros((S, E), flat.dtype).at[jnp.arange(S)[:, None], topi].set(topv)
        h = _swiglu(flat @ W1_shared)
        routed = jnp.zeros_like(shared)
        for e in range(E):
            routed = routed + h @ W2_experts[e] * w[:, e:e + 1]
        out = x + (shared + routed).reshape(Bb, Tt, C)
        return _rmsnorm(out, norm2_w)
    x = L0_attn_x
    x = x + 0.5 * _L0_ffn_ref(_layernorm(x, axis=-1), L0_ffn_Wq, L0_ffn_Wk_c, L0_ffn_Wv_c, L0_ffn_Wk, L0_ffn_Wv, L0_ffn_Wo, L0_ffn_W_shared_in, L0_ffn_W_shared_out, L0_ffn_W1_shared, L0_ffn_W2_experts, L0_ffn_Wg_gate, L0_ffn_We_gate, L0_ffn_group_bias, L0_ffn_expert_bias, L0_ffn_norm1_w, L0_ffn_norm2_w)
    x = x + _L0_attn_ref(_layernorm(x, axis=-1), L0_attn_Wq, L0_attn_Wk, L0_attn_Wv, L0_attn_Wo, L0_attn_bo)
    x = x + 0.5 * _L0_ffn_ref(_layernorm(x, axis=-1), L0_ffn_Wq, L0_ffn_Wk_c, L0_ffn_Wv_c, L0_ffn_Wk, L0_ffn_Wv, L0_ffn_Wo, L0_ffn_W_shared_in, L0_ffn_W_shared_out, L0_ffn_W1_shared, L0_ffn_W2_experts, L0_ffn_Wg_gate, L0_ffn_We_gate, L0_ffn_group_bias, L0_ffn_expert_bias, L0_ffn_norm1_w, L0_ffn_norm2_w)
    return x

_drawn_inputs = setup_inputs


def setup_inputs(seed=0):
    import zlib

    import numpy as np

    out = dict(_drawn_inputs(seed))
    spreads = {'L0_attn_bo': (0.0, 0.1),
     'L0_ffn_group_bias': (0.0, 0.8),
     'L0_ffn_expert_bias': (0.0, 0.8),
     'L0_ffn_norm1_w': (1.0, 0.2),
     'L0_ffn_norm2_w': (1.0, 0.2)}
    factors = {'L0_attn_Wq': 8.0,
     'L0_attn_Wk': 8.0,
     'L0_attn_Wv': 8.0,
     'L0_attn_Wo': 8.0,
     'L0_ffn_Wq': 8.0,
     'L0_ffn_Wk_c': 8.0,
     'L0_ffn_Wv_c': 8.0,
     'L0_ffn_Wk': 8.0,
     'L0_ffn_Wv': 8.0,
     'L0_ffn_Wo': 8.0,
     'L0_ffn_W_shared_in': 8.0,
     'L0_ffn_W_shared_out': 8.0,
     'L0_ffn_W1_shared': 8.0,
     'L0_ffn_W2_experts': 8.0,
     'L0_ffn_Wg_gate': 8.0,
     'L0_ffn_We_gate': 8.0}
    for name, (base, spread) in spreads.items():
        noise = np.random.default_rng([zlib.crc32(name.encode()), seed]).standard_normal(out[name].shape)
        drawn = base * np.exp(spread * noise) if base else spread * noise
        out[name] = jnp.asarray(drawn.astype(out[name].dtype))
    for name, factor in factors.items():
        out[name] = (out[name] * factor).astype(out[name].dtype)
    return out
```

```python
from contextlib import ExitStack

import concourse.bass as bass
from concourse import mybir
import numpy as np

F32 = mybir.dt.float32
BF16 = mybir.dt.bfloat16
ALU = mybir.AluOpType
ACT = mybir.ActivationFunctionType
AX = mybir.AxisListType

B, S, C = 4, 512, 128
TT = S // 128
H = 16
HP = H // 2
G4 = H // 4
LAYERS = 3
UNITS = LAYERS * B
E_GRP, EPG = 2, 4
E = E_GRP * EPG
HID = 256
DC = 32
LN_EPS, RMS_EPS = 1e-5, 1e-6
PARTS = 3
Q_PART = {8: (0, 0, 0, 1, 1, 2), 4: (0, 0, 0, 1, 1, 1, 2, 2, 2)}
K_PART = {8: (0, 1, 2, 0, 1, 0), 4: (0, 1, 2, 0, 1, 2, 0, 1, 2)}
VW = 32
ONE_COL = 8
AUG_RING = 3
P_RING = 3


def is_ffn(u):
    return u // B != 1


def ffn_index(u):
    return u if u < B else (B if u < 2 * B else u - B)


def before(u):
    return u - 1 if is_ffn(u - 1) else u - 1 - B


def head_dim(u):
    return C // H if is_ffn(u) else C // 2 // H


def product_rows(u):
    return head_dim(u) * len(Q_PART[head_dim(u)])


def stack_dmas(u):
    return 2 * 2 * len(Q_PART[head_dim(u)]) + 2


class Banks:

    def __init__(self):
        self.uses = [0, 0]
        self.last = 1

    def one(self):
        self.last ^= 1
        self.uses[self.last] += 1
        return [(self.last, self.uses[self.last] - 1)]

    def two(self):
        return self.one() + self.one()


def prep_steps(u):
    return [(1, ("norm_stats", u)), (3, ("norm_apply", u)), (5, ("x_transpose", u)), (7, ("qk_project", u, 0)),
            (7, ("qk_split", u, 0)), (9, ("v_project", u)), (12, ("qk_project", u, 1)), (12, ("qk_split", u, 1)),
            (20, ("stack", u))]


def post_steps(u):
    steps = [(0, ("heads_out", u)), (2, ("heads_transpose", u)), (4, ("out_project", u))]
    if not is_ffn(u):
        return steps + [(4, ("unit_out", u))]
    steps += [(5, ("rms_stats", u, 0)), (7, ("rms_apply1", u)), (9, ("x1_transpose", u)), (11, ("logits", u))]
    steps += [(11 + 2 * c, ("mlp_up", u, c)) for c in range(4)]
    steps += [(12 + k, ("router", u, k)) for k in range(8)]
    steps += [(19, ("shared_out", u))]
    steps += [(20 + 2 * t + half, ("expert", u, t, half)) for t in range(TT) for half in range(2)]
    steps += [(29, ("rms_stats", u, 1)), (30, ("rms_apply2", u)), (31, ("unit_out", u))]
    return steps


ONE_BANK = {"x_transpose", "v_project", "heads_transpose", "out_project", "x1_transpose", "logits", "shared_out",
            "expert", "max_rows"}
TWO_BANKS = {"heads_out", "mlp_up"}


def plan():
    order = []
    n_sub = 32
    for t in range(-2, UNITS + 1):
        core = [[] for _ in range(n_sub)]
        if 0 <= t + 1 < UNITS:
            for i in range(n_sub):
                core[i].append(("max_scores", t + 1, i // TT, i % TT))
            core[n_sub // 2 - 1].append(("max_parts", t + 1, 0))
            core[n_sub // 2 + 2].append(("max_rows", t + 1, 0))
            core[n_sub - 1].append(("max_parts", t + 1, 1))
        if 0 <= t < UNITS:
            for s in range(n_sub // 2):
                for j in range(2):
                    core[2 * s + j].insert(0, ("exp_scores", t, s, j))
                if s:
                    core[2 * s].insert(1, ("weigh_v", t, s - 1))
                    if (s - 1) % TT == TT - 1:
                        core[2 * s].append(("heads_evacuate", t, (s - 1) // TT))
            core[n_sub - 1] += [("weigh_v", t, n_sub // 2 - 1), ("heads_evacuate", t, G4 - 1)]
            core[4].append(("max_rows", t, 1))
        side = []
        if 0 <= t - 1:
            side += post_steps(t - 1)
        if t + 2 < UNITS:
            side += prep_steps(t + 2)
        for i in range(n_sub):
            order += core[i] + [step for place, step in side if place == i]
    banks = Banks()
    out = []
    for step in order:
        name, u = step[0], step[1]
        if name in TWO_BANKS or (name == "qk_project" and is_ffn(u)):
            use = banks.two()
        elif name in ONE_BANK or name == "qk_project":
            use = banks.one()
        else:
            use = []
        out.append((name, u, step[2:], use))
    return out


def macaron(nc, x, w, out):
    steps = plan()
    with ExitStack() as ctx:
        def sb(name, shape, dt=F32):
            return ctx.enter_context(nc.sbuf_tensor(name, shape, dt))

        def sem(name):
            return ctx.enter_context(nc.semaphore(name))

        X = sb("X", [128, B, TT, C])
        src = sb("src", [128, B, TT, C])
        xT = sb("xT", [128, S])
        rope_c = sb("rope_c", [128, S])
        rope_s = sb("rope_s", [128, S])
        qf = sb("qf", [128, 2, S])
        rest = sb("rest", [128, S])
        parts = sb("parts", [128, 2, PARTS, S], BF16)
        q_aug = sb("q_aug", [128, AUG_RING, HP, S], BF16)
        k_aug = sb("k_aug", [128, AUG_RING, HP, S], BF16)
        v_aug = sb("v_aug", [128, AUG_RING, TT, H * VW])
        maxes = sb("maxes", [128, 2, 2, TT, 2, HP // 2])
        max_rest = sb("max_rest", [128, TT, 2, HP // 2])
        max_parts = sb("max_parts", [128, TT, 2, PARTS, HP // 2], BF16)
        maxT = sb("maxT", [2 * PARTS * HP // 2, S], BF16)
        probs = sb("probs", [128, P_RING, 4, S])
        heads = sb("heads", [128, G4, S])
        denom = sb("denom", [128, TT * H])
        attn = sb("attn", [128, TT, C])
        attnT = sb("attnT", [128, S])
        y = sb("y", [128, TT, C])
        squares = sb("squares", [128, TT, C])
        sums = sb("sums", [128, 2, TT])
        mean_var = sb("mean_var", [128, TT, 2])
        stats = sb("stats", [128, TT, 6])
        var_eps = sb("var_eps", [128, TT])
        rstd = sb("rstd", [128, TT])
        rms = sb("rms", [128, 2, TT])
        rms_in = sb("rms_in", [128, TT])
        x1 = sb("x1", [128, TT, C])
        x1T = sb("x1T", [128, S])
        tanh = sb("tanh", [128, S])
        gated = sb("gated", [128, S])
        hidden = sb("hidden", [128, 4, S])
        acc = sb("acc", [128, TT, C])
        prod = sb("prod", [128, 2, EPG, C])
        psum2 = sb("psum2", [128, EPG, C])
        norm_out = sb("norm_out", [128, TT, C])
        logit = sb("logit", [128, TT, E_GRP + E])
        g_diff = sb("g_diff", [128, TT, 1])
        second = sb("second", [128, TT, 1])
        first = sb("first", [128, TT, 1])
        g_sign = sb("g_sign", [128, TT, 1])
        e_in = sb("e_in", [128, TT, EPG])
        e_tmp = sb("e_tmp", [128, TT, EPG])
        e_max = sb("e_max", [128, TT, 1])
        z = sb("z", [128, TT, EPG + 1])
        ez = sb("ez", [128, TT, EPG + 1])
        e_sum = sb("e_sum", [128, TT, 1])
        g_den = sb("g_den", [128, TT, 1])
        e_den = sb("e_den", [128, TT, 1])
        e_rden = sb("e_rden", [128, TT, 1])
        beaten = sb("beaten", [128, TT, EPG])
        above = sb("above", [128, TT, EPG])
        e_w = sb("e_w", [128, TT, EPG])
        gate = sb("gate", [128, TT, E])
        wq = sb("wq", [128, 2, C])
        wk = sb("wk", [128, 2, C])
        wv = sb("wv", [128, C])
        wo = sb("wo", [128, C])
        kcT = sb("kcT", [DC, 2, C])
        kv2 = sb("kv2", [DC, 2, C])
        awq = sb("awq", [C // 2, 3, C // 2])
        awo = sb("awo", [C // 2, C])
        w_in = sb("w_in", [128, 2, 2 * HID])
        w_out = sb("w_out", [128, 2, C])
        w2 = sb("w2", [128, 2, E, C])
        w_gate = sb("w_gate", [128, E_GRP + E])
        b_gate = sb("b_gate", [128, 1, E_GRP + E])
        bo = sb("bo", [128, 1, C])
        n1 = sb("n1", [128, C])
        n2 = sb("n2", [128, C])
        cosT = sb("cosT", [128, S])
        sinT = sb("sinT", [128, S])
        ident = sb("ident", [128, 128])
        identb = sb("identb", [128, 128], BF16)
        pick = {8: sb("pick8", [128, 4 * 9]), 4: sb("pick4", [128, 4 * 5])}
        power = sb("power", [128, TT])
        ones_row = sb("ones_row", [PARTS, 1, S], BF16)
        order0 = sb("order0", [128, TT, EPG])

        ps_max = ctx.enter_context(nc.psum_tensor("ps_max", [128, 2, S], F32))
        ps_exp = ctx.enter_context(nc.psum_tensor("ps_exp", [128, 2, S], F32))
        ps_out = ctx.enter_context(nc.psum_tensor("ps_out", [128, 2, S], F32))
        ps = ctx.enter_context(nc.psum_tensor("ps", [128, 2, S], F32))

        scratch = nc.dram_tensor("qk_parts", [2, 2, PARTS, C, S], BF16, kind="Internal").ap()
        scratch_max = nc.dram_tensor("max_parts_rows", [2, 2, PARTS, HP // 2, S], BF16, kind="Internal").ap()

        const_loaded = sem("const_loaded")
        x_loaded = sem("x_loaded")
        fused_done = sem("fused_done")
        fused_copied = sem("fused_copied")
        setup_pool = sem("setup_pool")
        pool_seq = sem("pool_seq")
        dve_seq = sem("dve_seq")
        bank_full = [sem("bank_full0"), sem("bank_full1")]
        bank_free = [sem("bank_free0"), sem("bank_free1")]
        stats_done = sem("stats_done")
        rstd_done = sem("rstd_done")
        src_done = sem("src_done")
        rope_used = sem("rope_used")
        part_done = sem("part_done")
        parts_stored = sem("parts_stored")
        aug_loaded = [sem(f"aug_loaded{i}") for i in range(AUG_RING)]
        max_full = sem("max_full")
        max_done = sem("max_done")
        max_split = sem("max_split")
        maxT_stored = sem("maxT_stored")
        max_loaded = [sem("max_loaded0"), sem("max_loaded1")]
        exp_full = sem("exp_full")
        exp_done = sem("exp_done")
        out_done = sem("out_done")
        heads_done = sem("heads_done")
        sums_done = sem("sums_done")
        rms_done = sem("rms_done")
        x1_done = sem("x1_done")
        router_pool = sem("router_pool")
        router_dve = sem("router_dve")
        router_act = sem("router_act")
        tanh_done = sem("tanh_done")
        expert_added = sem("expert_added")
        norm_done = sem("norm_done")
        x_done = sem("x_done")
        stored = sem("stored")

        consts = [
            (wq[:, 0, :], w["ffn_Wq"]), (wo[:, :], w["ffn_Wo"]),
            (kcT[:, 0, :], w["ffn_Wk_cT"]), (kcT[:, 1, :], w["ffn_Wv_cT"]),
            (kv2[:, 0, :], w["ffn_Wk"]), (kv2[:, 1, :], w["ffn_Wv"]),
            (awq[:, 0, :], w["attn_WqT"]), (awq[:, 1, :], w["attn_WkT"]), (awq[:, 2, :], w["attn_WvT"]),
            (awo[:, :], w["attn_WoT"]),
            (w_in[:, 0, :], w["ffn_W_shared_in"]), (w_in[:, 1, :], w["ffn_W1_shared"]),
            (w_out[:, :, :], w["ffn_W_shared_out"].rearrange("(k p) n -> p k n", p=128)),
            (w2[:, 0, :, :], w["ffn_W2_experts"][:, 0:128, :].rearrange("e p n -> p e n")),
            (w2[:, 1, :, :], w["ffn_W2_experts"][:, 128:256, :].rearrange("e p n -> p e n")),
            (w_gate[:, 0:E_GRP], w["ffn_Wg_gate"]), (w_gate[:, E_GRP:], w["ffn_We_gate"]),
            (b_gate[:, 0, 0:E_GRP], w["ffn_group_bias"].partition_broadcast(128)),
            (b_gate[:, 0, E_GRP:], w["ffn_expert_bias"].partition_broadcast(128)),
            (bo[:, 0, :], w["attn_bo"].partition_broadcast(128)),
            (n1[:, :], w["ffn_norm1_w"].partition_broadcast(128)),
            (n2[:, :], w["ffn_norm2_w"].partition_broadcast(128)),
            (cosT[:, :], w["cosT"]), (sinT[:, :], w["sinT"]),
            (ident[:, :], w["ident"]), 
            (pick[8][:, :], w["pick8"]), (pick[4][:, :], w["pick4"]),
        ]
        CONST = 16 * len(consts)
        scale = float(np.float32(1) / np.sqrt(np.float32(C // H)))

        uses = {(name, u, *args): use for name, u, args, use in steps}

        def pe_done(engine, *step):
            i, n = uses[step][-1]
            engine.wait_ge(bank_full[i], n + 1)

        def stacked(engine, u):
            engine.wait_ge(aug_loaded[u % AUG_RING], 16 * sum(stack_dmas(v) for v in range(u % AUG_RING, u + 1, AUG_RING)))

        def taken(engine, *step):
            for i, n in uses[step]:
                engine.wait_ge(bank_free[i], n + 1)

        block = ctx.enter_context(nc.Block())

        @block.sync
        def _(sp):
            sp.wait_ge(setup_pool, 1)
            for b in range(B):
                sp.dma_start(X[:, b, :, :], x[b].rearrange("(t p) c -> p t c", p=128)).then_inc(x_loaded, 16)
            for to, of in consts:
                sp.dma_start(to, of).then_inc(const_loaded, 16)
            for name, u, args, use in steps:
                d, r, f = head_dim(u), u % AUG_RING, ffn_index(u)
                rows = H * d
                if name == "qk_split":
                    qk, = args
                    if u >= 2 and qk == 0:
                        stacked(sp, u - 2)
                    sp.wait_ge(part_done, PARTS * (2 * u + qk + 1))
                    sp.dma_start(scratch[u % 2, qk, :, 0:rows, :].rearrange("c p n -> p c n"),
                                 parts[0:rows, qk, :, :]).then_inc(parts_stored, 16)
                elif name == "stack":
                    sp.wait_ge(parts_stored, 16 * 2 * (u + 1))
                    if u >= AUG_RING:
                        sp.wait_ge(exp_full, 32 * (u - AUG_RING + 1))
                    for qk, (aug, part_of) in enumerate(((q_aug, Q_PART[d]), (k_aug, K_PART[d]))):
                        v = scratch[u % 2, qk, :, 0:rows, :].rearrange("c (h r d) n -> c r d h n", r=2, d=d)
                        for par in range(2):
                            for s in range(len(part_of)):
                                p0 = 64 * par + d * s
                                sp.dma_start(aug[p0:p0 + d, r, :, :], v[part_of[s], par]).then_inc(aug_loaded[r], 16)
                    for par in range(2):
                        p0 = 64 * par + product_rows(u)
                        sp.dma_start(k_aug[p0:p0 + PARTS, r, :, :], ones_row[:, :, :].to_broadcast([PARTS, HP, S])).then_inc(aug_loaded[r], 16)
                elif name == "max_rows":
                    half, = args
                    taken(sp, "max_rows", u, half)
                    if u:
                        sp.wait_ge(max_loaded[half], 32 * u)
                    sp.dma_start(scratch_max[half].rearrange("r c h n -> (r c h) n"), maxT[:, :]).then_inc(maxT_stored, 16)
                    sp.wait_ge(maxT_stored, 16 * (2 * u + half + 1))
                    for par in range(2):
                        p0 = 64 * par + product_rows(u)
                        sp.dma_start(q_aug[p0:p0 + PARTS, r, half * HP // 2:(half + 1) * HP // 2, :],
                                     scratch_max[half, par]).then_inc(max_loaded[half], 16)
                elif name == "unit_out" and u // B == LAYERS - 1:
                    b = u % B
                    sp.wait_ge(x_done, u + 1)
                    sp.dma_start(out[b].rearrange("(t p) c -> p t c", p=128), X[:, b, :, :]).then_inc(stored, 16)
            sp.wait_ge(stored, 16 * B)

        @block.tensor
        def _(pe):
            def bank(use):
                i, n = use
                if n:
                    pe.wait_ge(bank_free[i], n)
                return ps[:, i, :]

            pe.wait_ge(const_loaded, CONST)
            for i in range(2):
                pe.matmul(ps_out[:, i, 0:C], kcT[:, i, :], kv2[:, i, :], start=True, stop=True).then_inc(fused_done, 1)
            pe.wait_ge(fused_copied, 1)
            pe.wait_ge(setup_pool, 1)
            for name, u, args, use in steps:
                d, r, b, f, ffn = head_dim(u), u % AUG_RING, u % B, ffn_index(u), is_ffn(u)
                rows = H * d
                if name == "x_transpose":
                    pe.wait_ge(src_done, u + 1)
                    o = bank(use[0])
                    for t in range(TT):
                        mm = pe.transpose(o[0:rows, t * 128:(t + 1) * 128], src[:, b, t, 0:rows], ident[:, :])
                    mm.then_inc(bank_full[use[0][0]], 1)
                elif name == "qk_project":
                    qk, = args
                    taken(pe, "x_transpose", u)
                    if ffn:
                        for i in range(2):
                            o = bank(use[i])
                            pe.matmul(o, (wq, wk)[qk][:, i, :], xT[:, :], start=True, stop=True)\
                              .then_inc(bank_full[use[i][0]], 1)
                    else:
                        pe.matmul(bank(use[0])[0:rows, :], awq[:, qk, :], xT[0:rows, :], start=True, stop=True)\
                          .then_inc(bank_full[use[0][0]], 1)
                elif name == "v_project":
                    taken(pe, "x_transpose", u)
                    o = bank(use[0])
                    wv_ = wv[:, :] if ffn else awq[:, 2, :]
                    for t in range(TT):
                        mm = pe.matmul(o[:, t * rows:(t + 1) * rows], xT[0:rows, t * 128:(t + 1) * 128], wv_,
                                       start=True, stop=True)
                    mm.then_inc(bank_full[use[0][0]], 1)
                elif name == "max_scores":
                    hp, qt = args
                    n = u * 32 + hp * TT + qt
                    if hp == 0 and qt == 0:
                        stacked(pe, u)
                    if n:
                        pe.wait_ge(max_done, n)
                    for par in range(2):
                        p0, k = 64 * par, product_rows(u)
                        mm = pe.matmul(ps_max[:, par, :], q_aug[p0:p0 + k, r, hp, qt * 128:(qt + 1) * 128],
                                       k_aug[p0:p0 + k, r, hp, :], start=True, stop=True)
                    mm.then_inc(max_full, 1)
                elif name == "max_rows":
                    half, = args
                    pe.wait_ge(max_split, 2 * u + half + 1)
                    o = bank(use[0]).bitcast(BF16)
                    n = 2 * PARTS * HP // 2
                    for t in range(TT):
                        mm = pe.transpose(o[0:n, t * 128:(t + 1) * 128],
                                          max_parts[:, t, :, :, :].rearrange("p a c h -> p (a c h)"), identb[:, :])
                    mm.then_inc(bank_full[use[0][0]], 1)
                elif name == "exp_scores":
                    s, j = args
                    g, kt = s // TT, s % TT
                    hp, n = 2 * g + j, u * 32 + 2 * s + j
                    if hp % (HP // 2) == 0 and kt == 0:
                        pe.wait_ge(max_loaded[hp // (HP // 2)], 32 * (u + 1))
                    if n:
                        pe.wait_ge(exp_done, n)
                    for par in range(2):
                        p0, k = 64 * par, product_rows(u) + PARTS
                        mm = pe.matmul(ps_exp[:, par, :], k_aug[p0:p0 + k, r, hp, kt * 128:(kt + 1) * 128],
                                       q_aug[p0:p0 + k, r, hp, :], start=True, stop=True)
                    mm.then_inc(exp_full, 1)
                elif name == "weigh_v":
                    s, = args
                    g, kt, n = s // TT, s % TT, u * 16 + s
                    pe.wait_ge(exp_done, 2 * (n + 1))
                    if s == 0:
                        taken(pe, "v_project", u)
                    if kt == 0 and u * G4 + g >= 2:
                        pe.wait_ge(heads_done, u * G4 + g - 1)
                    for c in range(4):
                        h = 4 * g + c
                        mm = pe.matmul(ps_out[32 * c:32 * c + VW, g % 2, :], v_aug[:, r, kt, h * VW:(h + 1) * VW],
                                       probs[:, n % P_RING, c, :], start=(kt == 0), stop=(kt == TT - 1))
                    mm.then_inc(out_done, 1)
                elif name == "heads_out":
                    pe.wait_ge(heads_done, G4 * (u + 1))
                    cols = 4 * (d + 1)
                    for i in range(2):
                        o = bank(use[i])
                        for t in range(2):
                            for g in range(G4):
                                c0 = (t * G4 + g) * cols
                                mm = pe.matmul(o[:, c0:c0 + cols],
                                               heads[:, g, (2 * i + t) * 128:(2 * i + t + 1) * 128],
                                               pick[d][:, :], start=True, stop=True)
                        mm.then_inc(bank_full[use[i][0]], 1)
                elif name == "heads_transpose":
                    taken(pe, "heads_out", u)
                    o = bank(use[0])
                    for t in range(TT):
                        mm = pe.transpose(o[0:rows, t * 128:(t + 1) * 128], attn[:, t, 0:rows], ident[:, :])
                    mm.then_inc(bank_full[use[0][0]], 1)
                elif name == "out_project":
                    taken(pe, "heads_transpose", u)
                    o = bank(use[0])
                    for t in range(TT):
                        mm = pe.matmul(o[:, t * C:(t + 1) * C], attnT[0:rows, t * 128:(t + 1) * 128],
                                       wo[:, :] if ffn else awo[:, :], start=True, stop=True)
                    mm.then_inc(bank_full[use[0][0]], 1)
                elif name == "x1_transpose":
                    pe.wait_ge(x1_done, f + 1)
                    o = bank(use[0])
                    for t in range(TT):
                        mm = pe.transpose(o[:, t * 128:(t + 1) * 128], x1[:, t, :], ident[:, :])
                    mm.then_inc(bank_full[use[0][0]], 1)
                elif name == "logits":
                    taken(pe, "x1_transpose", u)
                    o, n = bank(use[0]), E_GRP + E
                    for t in range(TT):
                        mm = pe.matmul(o[:, t * n:(t + 1) * n], x1T[:, t * 128:(t + 1) * 128], w_gate[:, :],
                                       start=True, stop=True)
                    mm.then_inc(bank_full[use[0][0]], 1)
                elif name == "mlp_up":
                    c, = args
                    taken(pe, "x1_transpose", u)
                    for i in range(2):
                        c0 = i * HID + (c % 2) * 128
                        pe.matmul(bank(use[i]), w_in[:, c // 2, c0:c0 + 128], x1T[:, :], start=True, stop=True)\
                          .then_inc(bank_full[use[i][0]], 1)
                elif name == "shared_out":
                    taken(pe, "mlp_up", u, 1)
                    o = bank(use[0])
                    for t in range(TT):
                        for k in range(2):
                            mm = pe.matmul(o[:, t * C:(t + 1) * C], hidden[:, k, t * 128:(t + 1) * 128],
                                           w_out[:, k, :], start=(k == 0), stop=(k == 1))
                    mm.then_inc(bank_full[use[0][0]], 1)
                elif name == "expert":
                    t, half = args
                    taken(pe, "mlp_up", u, 3)
                    o = bank(use[0])
                    for k in range(2):
                        mm = pe.matmul(o, hidden[:, 2 + k, t * 128:(t + 1) * 128],
                                       w2[:, k, half * EPG:(half + 1) * EPG, :].rearrange("p e n -> p (e n)"),
                                       start=(k == 0), stop=(k == 1))
                    mm.then_inc(bank_full[use[0][0]], 1)

        @block.vector
        def _(dve):
            own = [0]

            def seq(ins):
                own[0] += 1
                ins.then_inc(dve_seq, 1)

            def own_wait():
                dve.wait_ge(dve_seq, own[0])

            def full(use):
                i, n = use
                dve.wait_ge(bank_full[i], n + 1)
                return ps[:, i, :]

            dve.wait_ge(const_loaded, CONST)
            dve.wait_ge(fused_done, 2)
            seq(dve.tensor_copy(wk[:, 0, :], ps_out[:, 0, 0:C]))
            own_wait()
            for t in (wq, wk):
                plain = t[:, 0, :].rearrange("p (i e) -> p i e", e=2)
                turned = t[:, 1, :].rearrange("p (i e) -> p i e", e=2)
                seq(dve.tensor_scalar(turned[:, :, 0], plain[:, :, 1], -1.0, None, ALU.mult))
                seq(dve.tensor_copy(turned[:, :, 1], plain[:, :, 0]))
            seq(dve.tensor_copy(identb[:, :], ident[:, :]))
            seq(dve.tensor_scalar(n2[:, :], n2[:, :], 0.5, None, ALU.mult))
            own_wait()
            dve.tensor_copy(wv[:, :], ps_out[:, 1, 0:C]).then_inc(fused_copied, 1)
            dve.wait_ge(x_loaded, 16 * B)
            for name, u, args, use in steps:
                d, r, b, f, ffn = head_dim(u), u % AUG_RING, u % B, ffn_index(u), is_ffn(u)
                rows = H * d
                if name == "norm_stats":
                    if u >= B:
                        dve.wait_ge(x_done, u - B + 1)
                    if u:
                        dve.wait_ge(src_done, u)
                    for t in range(TT):
                        seq(dve.bn_stats(stats[:, t, :], X[:, b, t, :]))
                    own_wait()
                    for t in range(TT):
                        ins = dve.bn_aggr(mean_var[:, t, :], stats[:, t, :])
                        if t < TT - 1:
                            seq(ins)
                    ins.then_inc(stats_done, 1)
                elif name == "norm_apply":
                    dve.wait_ge(rstd_done, u + 1)
                    own_wait()
                    dve.wait_ge(stats_done, u + 1)
                    if u >= B:
                        taken(dve, "x_transpose", u - B)
                    for t in range(TT):
                        ins = dve.tensor_scalar(src[:, b, t, :], X[:, b, t, :], mean_var[:, t, 0:1], rstd[:, t:t + 1],
                                                ALU.subtract, ALU.mult)
                    ins.then_inc(src_done, 1)
                elif name == "qk_project" and ffn:
                    qk, = args
                    if f + qk:
                        dve.wait_ge(rope_used, 2 * f + qk)
                    dve.tensor_tensor(rope_c[:, :], full(use[0]), cosT[:, :], ALU.mult).then_inc(bank_free[use[0][0]], 1)
                    ins = dve.tensor_tensor(rope_s[:, :], full(use[1]), sinT[:, :], ALU.mult)
                    ins.then_inc(bank_free[use[1][0]], 1)
                elif name == "max_scores":
                    hp, qt = args
                    n = u * 32 + hp * TT + qt
                    half, h2 = hp // (HP // 2), hp % (HP // 2)
                    if hp == 0 and qt == 0 and u >= 2:
                        dve.wait_ge(max_split, 2 * (u - 1))
                    dve.wait_ge(max_full, n + 1)
                    dve.tensor_reduce(maxes[:, u % 2, half, qt, :, h2:h2 + 1], ps_max[:, :, :], AX.X, ALU.max)\
                       .then_inc(max_done, 1)
                elif name == "heads_out":
                    tiles = [full(use[i])[:, 0:2 * H * (d + 1)].rearrange("p (h e) -> p h e", e=d + 1) for i in range(2)]
                    half = 2 * H
                    for i in range(2):
                        e = d
                        seq(dve.reciprocal(denom[:, i * half:(i + 1) * half].unsqueeze(2), tiles[i][:, :, e:e + 1]))
                    own_wait()
                    if u:
                        taken(dve, "heads_transpose", u - 1)
                    for i in range(2):
                        o = attn[:, 2 * i:2 * i + 2, 0:rows].rearrange("p t (h e) -> p t h e", e=d)
                        ins = dve.tensor_tensor(
                            o, tiles[i].rearrange("p (t h) e -> p t h e", t=2)[:, :, :, 0:d],
                            denom[:, i * half:(i + 1) * half].rearrange("p (t h) -> p t h", t=2).unsqueeze(3)
                            .to_broadcast([128, 2, H, d]), ALU.mult)
                        ins.then_inc(bank_free[use[i][0]], 1)
                elif name == "out_project":
                    o = full(use[0]).rearrange("p (t c) -> p t c", c=C)
                    if ffn:
                        if f:
                            dve.wait_ge(x1_done, f)
                            dve.wait_ge(sums_done, 2 * f)
                        ins = dve.tensor_tensor(y[:, :, :], o, src[:, b, :, :], ALU.add)
                        ins.then_inc(bank_free[use[0][0]], 1)
                    else:
                        ins = dve.tensor_tensor(X[:, b, :, :], o, X[:, b, :, :], ALU.add)
                        ins.then_inc(bank_free[use[0][0]], 1)
                elif name == "rms_apply1":
                    dve.wait_ge(rms_done, 2 * f + 1)
                    taken(dve, "out_project", u)
                    if f:
                        taken(dve, "shared_out", before(u))
                        taken(dve, "x1_transpose", before(u))
                    for t in range(TT):
                        ins = dve.scalar_tensor_tensor(out=x1[:, t, :], in0=y[:, t, :], scalar=rms[:, 0, t:t + 1],
                                                       in1=n1[:, :], op0=ALU.mult, op1=ALU.mult)
                    ins.then_inc(x1_done, 1)
                elif name == "logits":
                    if f:
                        dve.wait_ge(router_pool, 4 * f)
                    n = E_GRP + E
                    ins = dve.tensor_tensor(logit[:, :, :], full(use[0])[:, 0:TT * n].rearrange("p (t n) -> p t n", n=n),
                                            b_gate[:, :, :].to_broadcast([128, TT, n]), ALU.add)
                    ins.then_inc(bank_free[use[0][0]], 1)
                elif name == "router":
                    k, = args
                    if k == 1:
                        dve.wait_ge(router_pool, 4 * f + 1)
                        dve.tensor_reduce(e_max[:, :, :], e_in[:, :, :], AX.X, ALU.max).then_inc(router_dve, 1)
                    elif k == 4:
                        dve.wait_ge(router_act, f + 1)
                        dve.tensor_reduce(e_sum[:, :, :], ez[:, :, 0:EPG], AX.X, ALU.add).then_inc(router_dve, 1)
                    elif k == 6:
                        dve.wait_ge(router_pool, 4 * f + 3)
                        dve.reciprocal(e_rden[:, :, :], e_den[:, :, :]).then_inc(router_dve, 1)
                elif name == "mlp_up":
                    c, = args
                    if f:
                        pe_done(dve, *(("shared_out", before(u)) if c < 2 else ("expert", before(u), TT - 1, 1)))
                    dve.wait_ge(tanh_done, 4 * f + c + 1)
                    ins = dve.scalar_tensor_tensor(out=gated[:, :], in0=tanh[:, :], scalar=1.0, in1=full(use[0]),
                                                   op0=ALU.add, op1=ALU.mult)
                    ins.then_inc(bank_free[use[0][0]], 1)
                    dve.wait_ge(bank_free[use[0][0]], use[0][1] + 1)
                    ins = dve.scalar_tensor_tensor(out=hidden[:, c, :], in0=gated[:, :], scalar=0.5, in1=full(use[1]),
                                                   op0=ALU.mult, op1=ALU.mult)
                    ins.then_inc(bank_free[use[1][0]], 1)
                elif name == "shared_out":
                    if f:
                        dve.wait_ge(norm_done, f)
                        dve.wait_ge(sums_done, 2 * f)
                    dve.wait_ge(x1_done, f + 1)
                    ins = dve.tensor_tensor(acc[:, :, :], full(use[0]).rearrange("p (t c) -> p t c", c=C), x1[:, :, :],
                                            ALU.add)
                    ins.then_inc(bank_free[use[0][0]], 1)
                elif name == "expert":
                    t, half = args
                    n = (f * TT + t) * 2 + half
                    dve.wait_ge(router_pool, 4 * (f + 1))
                    if n >= 2:
                        dve.wait_ge(expert_added, n // 2)
                    ins = dve.tensor_tensor(prod[:, half, :, :], full(use[0]).rearrange("p (e c) -> p e c", c=C),
                                            gate[:, t, half * EPG:(half + 1) * EPG].unsqueeze(2)
                                            .to_broadcast([128, EPG, C]), ALU.mult)
                    ins.then_inc(bank_free[use[0][0]], 1)
                elif name == "rms_apply2":
                    dve.wait_ge(rms_done, 2 * f + 2)
                    dve.wait_ge(expert_added, TT * (f + 1))
                    if f:
                        dve.wait_ge(x_done, u)
                    for t in range(TT):
                        ins = dve.scalar_tensor_tensor(out=norm_out[:, t, :], in0=acc[:, t, :],
                                                       scalar=rms[:, 1, t:t + 1], in1=n2[:, :],
                                                       op0=ALU.mult, op1=ALU.mult)
                    ins.then_inc(norm_done, 1)

        @block.scalar
        def _(act):
            def full(use):
                i, n = use
                act.wait_ge(bank_full[i], n + 1)
                return ps[:, i, :]

            act.wait_ge(setup_pool, 1)
            for name, u, args, use in steps:
                d, r, b, f, ffn = head_dim(u), u % AUG_RING, u % B, ffn_index(u), is_ffn(u)
                rows = H * d
                if name == "x_transpose":
                    if u:
                        pe_done(act, "v_project", u - 1)
                    ins = act.activation(xT[0:rows, :], full(use[0])[0:rows, :], ACT.Copy)
                    ins.then_inc(bank_free[use[0][0]], 1)
                elif name == "qk_project" and not ffn:
                    qk, = args
                    act.wait_ge(part_done, PARTS * (2 * (u - 1) + qk + 1))
                    ins = act.activation(qf[0:rows, qk, :], full(use[0])[0:rows, :], ACT.Copy)
                    ins.then_inc(bank_free[use[0][0]], 1)
                elif name == "v_project":
                    if u >= AUG_RING:
                        act.wait_ge(out_done, 16 * (u - AUG_RING + 1))
                    to = v_aug[:, r, :, :].rearrange("p t (h e) -> p (t h) e", e=VW)[:, :, 0:d]
                    ins = act.activation(to, full(use[0])[:, 0:TT * rows].rearrange("p (m e) -> p m e", e=d), ACT.Copy)
                    ins.then_inc(bank_free[use[0][0]], 1)
                elif name == "max_rows":
                    half, = args
                    if u + half:
                        act.wait_ge(maxT_stored, 16 * (2 * u + half))
                    n = 2 * PARTS * HP // 2
                    ins = act.activation(maxT[:, :], full(use[0]).bitcast(BF16)[0:n, 0:S], ACT.Copy)
                    ins.then_inc(bank_free[use[0][0]], 1)
                elif name == "exp_scores":
                    s, j = args
                    n = u * 32 + 2 * s + j
                    act.wait_ge(exp_full, n + 1)
                    if j == 0 and n // 2 >= P_RING:
                        act.wait_ge(out_done, n // 2 - P_RING + 1)
                    act.activation(probs[:, (n // 2) % P_RING, 2 * j:2 * j + 2, :], ps_exp[:, :, :], ACT.Exp,
                                   scale=scale).then_inc(exp_done, 1)
                elif name == "heads_evacuate":
                    g, = args
                    act.wait_ge(out_done, u * 16 + TT * (g + 1))
                    if u:
                        pe_done(act, "heads_out", u - 1)
                    act.activation(heads[:, g, :], ps_out[:, g % 2, :], ACT.Copy).then_inc(heads_done, 1)
                elif name == "heads_transpose":
                    if u:
                        pe_done(act, "out_project", u - 1)
                    ins = act.activation(attnT[0:rows, :], full(use[0])[0:rows, :], ACT.Copy)
                    ins.then_inc(bank_free[use[0][0]], 1)
                elif name == "rms_stats":
                    which, = args
                    of = (y, acc)[which]
                    if which == 0:
                        taken(act, "out_project", u)
                    else:
                        act.wait_ge(expert_added, TT * (f + 1))
                    if f + which:
                        act.wait_ge(sums_done, 2 * f + which)
                    if f:
                        act.wait_ge(rms_done, 2 * f - 1 + which)
                    for t in range(TT):
                        ins = act.activation(squares[:, t, :], of[:, t, :], ACT.Square, accum_out=sums[:, which, t:t + 1])
                    ins.then_inc(sums_done, 1)
                elif name == "x1_transpose":
                    if f:
                        pe_done(act, "mlp_up", before(u), 3)
                    ins = act.activation(x1T[:, :], full(use[0]), ACT.Copy)
                    ins.then_inc(bank_free[use[0][0]], 1)
                elif name == "router" and args[0] == 3:
                    act.wait_ge(router_pool, 4 * f + 2)
                    act.activation(ez[:, :, :], z[:, :, :], ACT.Exp).then_inc(router_act, 1)
                elif name == "mlp_up":
                    c, = args
                    if f + c:
                        taken(act, "mlp_up", u if c else before(u), (c - 1) % 4)
                    act.activation(tanh[:, :], full(use[0]), ACT.Tanh, scale=0.5).then_inc(tanh_done, 1)

        @block.gpsimd
        def _(pool):
            own = [0]

            def seq(ins):
                own[0] += 1
                ins.then_inc(pool_seq, 1)
                return ins

            def own_wait():
                pool.wait_ge(pool_seq, own[0])

            seq(pool.memset(v_aug[:, :, :, :], 0.0))
            seq(pool.memset(power[:, :], -0.5))
            seq(pool.memset(ones_row[:, :, :], 1.0))
            for e in range(EPG):
                seq(pool.memset(order0[:, :, e:e + 1], float(e)))
            own_wait()
            ones = v_aug[:, :, :, :].rearrange("p r t (h e) -> p (r t h) e", e=VW)[:, :, ONE_COL:ONE_COL + 1]
            pool.memset(ones, 1.0).then_inc(setup_pool, 1)
            pool.wait_ge(const_loaded, CONST)
            for name, u, args, use in steps:
                d, r, b, f, ffn = head_dim(u), u % AUG_RING, u % B, ffn_index(u), is_ffn(u)
                rows = H * d
                if name == "norm_stats":
                    pool.wait_ge(stats_done, u + 1)
                    seq(pool.tensor_scalar(var_eps[:, :].unsqueeze(2), mean_var[:, :, 1:2], LN_EPS, None, ALU.add))
                    own_wait()
                    if u:
                        pool.wait_ge(src_done, u)
                    pool.tensor_tensor(rstd[:, :], var_eps[:, :], power[:, :], ALU.pow).then_inc(rstd_done, 1)
                elif name == "qk_split":
                    qk, = args
                    q = qf[0:rows, qk, :]
                    if ffn:
                        taken(pool, "qk_project", u, qk)
                        if u >= B:
                            pool.wait_ge(part_done, PARTS * (2 * (u - 1) + qk + 1))
                        ins = pool.tensor_tensor(q, rope_c[:, :], rope_s[:, :], ALU.add)
                        ins.then_inc(rope_used, 1)
                        pool.wait_ge(rope_used, 2 * f + qk + 1)
                    else:
                        taken(pool, "qk_project", u, qk)
                    if u:
                        pool.wait_ge(parts_stored, 16 * (2 * (u - 1) + qk + 1))
                    h, m, l = (parts[0:rows, qk, c, :] for c in range(PARTS))
                    n = PARTS * (2 * u + qk)
                    pool.tensor_copy(h, q).then_inc(part_done, 1)
                    pool.wait_ge(part_done, n + 1)
                    seq(pool.tensor_tensor(rest[0:rows, :], q, h, ALU.subtract))
                    own_wait()
                    pool.tensor_copy(m, rest[0:rows, :]).then_inc(part_done, 1)
                    pool.wait_ge(part_done, n + 2)
                    pool.tensor_tensor(l, rest[0:rows, :], m, ALU.subtract).then_inc(part_done, 1)
                elif name == "max_parts":
                    half, = args
                    pool.wait_ge(max_done, u * 32 + 16 * (half + 1))
                    if u + half:
                        pe_done(pool, "max_rows", *((u, 0) if half else (u - 1, 1)))
                    mx = maxes[:, u % 2, half, :, :, :]
                    h, m, l = (max_parts[:, :, :, c, :] for c in range(PARTS))
                    seq(pool.tensor_scalar(h, mx, -1.0, None, ALU.mult))
                    own_wait()
                    seq(pool.tensor_tensor(max_rest[:, :, :, :], mx, h, ALU.add))
                    own_wait()
                    seq(pool.tensor_scalar(m, max_rest[:, :, :, :], -1.0, None, ALU.mult))
                    own_wait()
                    seq(pool.tensor_tensor(max_rest[:, :, :, :], max_rest[:, :, :, :], m, ALU.add))
                    own_wait()
                    pool.tensor_scalar(l, max_rest[:, :, :, :], -1.0, None, ALU.mult).then_inc(max_split, 1)
                elif name == "rms_stats":
                    which, = args
                    pool.wait_ge(sums_done, 2 * f + which + 1)
                    seq(pool.tensor_scalar(rms_in[:, :], sums[:, which, :], 1.0 / C, RMS_EPS, ALU.mult, ALU.add))
                    own_wait()
                    if f:
                        pool.wait_ge((x1_done, norm_done)[which], f)
                    pool.tensor_tensor(rms[:, which, :], rms_in[:, :], power[:, :], ALU.pow).then_inc(rms_done, 1)
                elif name == "router":
                    k, = args
                    wide = [128, TT, EPG]
                    if k == 0:
                        taken(pool, "logits", u)
                        if f:
                            pool.wait_ge(router_dve, 3 * f)
                        seq(pool.tensor_tensor(g_diff[:, :, :], logit[:, :, 1:2], logit[:, :, 0:1], ALU.subtract))
                        own_wait()
                        seq(pool.tensor_scalar(second[:, :, :], g_diff[:, :, :], 0.0, None, ALU.is_gt))
                        own_wait()
                        seq(pool.tensor_scalar(first[:, :, :], second[:, :, :], -1.0, 1.0, ALU.mult, ALU.add))
                        seq(pool.tensor_tensor(e_tmp[:, :, :], logit[:, :, E_GRP + EPG:], second[:, :, :].to_broadcast(wide),
                                               ALU.mult))
                        own_wait()
                        seq(pool.tensor_tensor(e_in[:, :, :], logit[:, :, E_GRP:E_GRP + EPG],
                                               first[:, :, :].to_broadcast(wide), ALU.mult))
                        own_wait()
                        pool.tensor_tensor(e_in[:, :, :], e_in[:, :, :], e_tmp[:, :, :], ALU.add).then_inc(router_pool, 1)
                    elif k == 2:
                        pool.wait_ge(router_dve, 3 * f + 1)
                        seq(pool.tensor_tensor(z[:, :, 0:EPG], e_in[:, :, :], e_max[:, :, :].to_broadcast(wide),
                                               ALU.subtract))
                        seq(pool.tensor_tensor(g_sign[:, :, :], first[:, :, :], second[:, :, :], ALU.subtract))
                        own_wait()
                        pool.tensor_tensor(z[:, :, EPG:EPG + 1], g_diff[:, :, :], g_sign[:, :, :], ALU.mult)\
                            .then_inc(router_pool, 1)
                        seq(pool.tensor_copy(beaten[:, :, :], order0[:, :, :]))
                        for s in range(1, EPG):
                            lo, hi, n = slice(0, EPG - s), slice(s, EPG), EPG - s
                            seq(pool.tensor_tensor(above[:, :, 0:n], e_in[:, :, hi], e_in[:, :, lo], ALU.subtract))
                            own_wait()
                            seq(pool.tensor_scalar(above[:, :, 0:n], above[:, :, 0:n], 0.0, None, ALU.is_gt))
                            own_wait()
                            seq(pool.tensor_tensor(beaten[:, :, lo], beaten[:, :, lo], above[:, :, 0:n], ALU.add))
                            own_wait()
                            seq(pool.tensor_tensor(beaten[:, :, hi], beaten[:, :, hi], above[:, :, 0:n], ALU.subtract))
                            own_wait()
                        seq(pool.tensor_scalar(beaten[:, :, :], beaten[:, :, :], 1.5, None, ALU.is_lt))
                    elif k == 5:
                        pool.wait_ge(router_dve, 3 * f + 2)
                        seq(pool.tensor_scalar(g_den[:, :, :], ez[:, :, EPG:EPG + 1], 1.0, None, ALU.add))
                        own_wait()
                        pool.tensor_tensor(e_den[:, :, :], e_sum[:, :, :], g_den[:, :, :], ALU.mult)\
                            .then_inc(router_pool, 1)
                        seq(pool.tensor_tensor(e_w[:, :, :], ez[:, :, 0:EPG], beaten[:, :, :], ALU.mult))
                    elif k == 7:
                        pool.wait_ge(router_dve, 3 * f + 3)
                        own_wait()
                        seq(pool.tensor_tensor(e_w[:, :, :], e_w[:, :, :], e_rden[:, :, :].to_broadcast(wide), ALU.mult))
                        own_wait()
                        if f:
                            taken(pool, "expert", before(u), TT - 1, 1)
                        seq(pool.tensor_tensor(gate[:, :, 0:EPG], e_w[:, :, :], first[:, :, :].to_broadcast(wide), ALU.mult))
                        own_wait()
                        pool.tensor_tensor(gate[:, :, EPG:], e_w[:, :, :], second[:, :, :].to_broadcast(wide), ALU.mult)\
                            .then_inc(router_pool, 1)
                elif name == "expert" and args[1] == 1:
                    t = args[0]
                    taken(pool, "expert", u, t, 0)
                    taken(pool, "expert", u, t, 1)
                    if t == 0:
                        taken(pool, "shared_out", u)
                    seq(pool.tensor_tensor(psum2[:, :, :], prod[:, 0, :, :], prod[:, 1, :, :], ALU.add))
                    own_wait()
                    seq(pool.tensor_tensor(psum2[:, 0:2, :], psum2[:, 0:2, :], psum2[:, 2:4, :], ALU.add))
                    own_wait()
                    seq(pool.tensor_tensor(acc[:, t, :], acc[:, t, :], psum2[:, 0, :], ALU.add))
                    own_wait()
                    pool.tensor_tensor(acc[:, t, :], acc[:, t, :], psum2[:, 1, :], ALU.add).then_inc(expert_added, 1)
                elif name == "unit_out":
                    if ffn:
                        pool.wait_ge(norm_done, f + 1)
                        if u >= B:
                            pool.wait_ge(x_done, u - B + 1)
                        pool.tensor_tensor(X[:, b, :, :], X[:, b, :, :], norm_out[:, :, :], ALU.add).then_inc(x_done, 1)
                    else:
                        taken(pool, "out_project", u)
                        pool.tensor_tensor(X[:, b, :, :], X[:, b, :, :], bo[:, :, :].to_broadcast([128, TT, C]), ALU.add)\
                            .then_inc(x_done, 1)


_PLAIN = ["ffn_Wq", "ffn_Wo", "ffn_Wk", "ffn_Wv", "ffn_W_shared_in", "ffn_W1_shared", "ffn_W_shared_out",
          "ffn_W2_experts", "ffn_Wg_gate", "ffn_We_gate", "ffn_group_bias", "ffn_expert_bias", "ffn_norm1_w",
          "ffn_norm2_w", "attn_bo"]
_TURNED = ["ffn_Wk_c", "ffn_Wv_c", "attn_Wq", "attn_Wk", "attn_Wv", "attn_Wo"]


def shape_constants():
    dh = C // H
    inv = (1.0 / np.power(np.float32(10000.0), np.arange(0, dh, 2, dtype=np.float32) / np.float32(dh))).astype(np.float32)
    ang = np.arange(S, dtype=np.float32)[:, None] * inv[None, :]
    rows = (np.arange(C) % dh) // 2
    out = {"cosT": np.cos(ang).T[rows], "sinT": np.sin(ang).T[rows], "ident": np.eye(128)}
    for d in (8, 4):
        pick = np.zeros((128, 4, d + 1))
        for c in range(4):
            for e in range(d):
                pick[VW * c + e, c, e] = 1
            pick[VW * c + ONE_COL, c, d] = 1
        out[f"pick{d}"] = pick.reshape(128, -1)
    out = {k: np.ascontiguousarray(v, dtype=np.float32) for k, v in out.items()}
    return out


def kernel(**inputs):
    import concourse.bacc as _bacc
    from concourse.bass_utils import run_bass_kernel_spmd as _run

    nc = _bacc.Bacc("TRN2", target_bir_lowering=False, num_devices=1)
    arrays = {"x": np.ascontiguousarray(inputs["L0_attn_x"])}
    for name in _PLAIN:
        arrays[name] = np.ascontiguousarray(inputs["L0_" + name])
    for name in _TURNED:
        arrays[name + "T"] = np.ascontiguousarray(np.transpose(inputs["L0_" + name]))
    arrays.update(shape_constants())
    aps, feed = {}, {}
    for name, a in arrays.items():
        feed[f"in_{name}_dram"] = a
        aps[name] = nc.dram_tensor(f"in_{name}_dram", a.shape, mybir.dt.from_np(a.dtype), kind="ExternalInput").ap()
    out = nc.dram_tensor("out_0_dram", (B, S, C), F32, kind="ExternalOutput").ap()
    macaron(nc, aps.pop("x"), aps, out)
    r = _run(nc, [feed], core_ids=[0])
    return r.results[0]["out_0_dram"]
```

```python
from contextlib import ExitStack

import concourse.bass as bass
from concourse import mybir
import numpy as np

F32 = mybir.dt.float32
BF16 = mybir.dt.bfloat16
ALU = mybir.AluOpType
ACT = mybir.ActivationFunctionType
AX = mybir.AxisListType

B, S, C = 4, 512, 128
TT = S // 128
H = 16
HH = H // 2
G4 = H // 4
LAYERS = 3
UNITS = LAYERS * B
E_GRP, EPG = 2, 4
E = E_GRP * EPG
HID = 256
DC = 32
LN_EPS, RMS_EPS = 1e-5, 1e-6
PARTS = 3
COL = 32
VW = 9
ONE_COL = 8
AUG_RING = 3
MAX_RING, EXP_RING = 3, 2
TILES = H * TT
MAX_LATE = 6
P_RING = 2


def is_ffn(u):
    return u // B != 1


def ffn_index(u):
    return u if u < B else (B if u < 2 * B else u - B)


def before(u):
    return u - 1 if is_ffn(u - 1) else u - 1 - B


def head_dim(u):
    return C // H if is_ffn(u) else C // 2 // H


def product_rows(u):
    return head_dim(u) * PARTS * PARTS


def stack_dmas(u):
    return 2 * PARTS * PARTS + 1 + (product_rows(u) < product_rows(0))


class Banks:

    def __init__(self):
        self.uses = [0, 0]
        self.last = 1

    def one(self):
        self.last ^= 1
        self.uses[self.last] += 1
        return [(self.last, self.uses[self.last] - 1)]

    def two(self):
        return self.one() + self.one()


def prep_steps(u):
    return [(1, ("norm_stats", u)), (3, ("norm_apply", u)), (5, ("x_transpose", u)), (7, ("qk_project", u, 0)),
            (7, ("qk_split", u, 0)), (9, ("v_project", u)), (12, ("qk_project", u, 1)), (12, ("qk_split", u, 1)),
            (20, ("stack", u))]


def post_steps(u):
    steps = [(t // 2, ("heads_out", u, t)) for t in range(TT)]
    steps += [(3, ("heads_transpose", u)), (4, ("out_project", u))]
    if not is_ffn(u):
        return steps + [(4, ("unit_out", u))]
    steps += [(5, ("rms_stats", u, 0)), (7, ("rms_apply1", u)), (9, ("x1_transpose", u)), (11, ("logits", u))]
    steps += [(11 + 2 * c, ("mlp_up", u, c)) for c in range(4)]
    steps += [(12 + k, ("router", u, k)) for k in range(8)]
    steps += [(19, ("shared_out", u))]
    steps += [(20 + 2 * t + half, ("expert", u, t, half)) for t in range(TT) for half in range(2)]
    steps += [(29, ("rms_stats", u, 1)), (30, ("rms_apply2", u)), (31, ("unit_out", u))]
    return steps


ONE_BANK = {"x_transpose", "v_project", "heads_transpose", "out_project", "x1_transpose", "logits", "shared_out",
            "expert", "max_rows", "heads_out"}
TWO_BANKS = {"mlp_up"}


def plan():
    order = []
    n_sub = 32
    first_place = -2 * n_sub
    places = [[] for _ in range((UNITS + 4) * n_sub)]

    def put(place, *step):
        places[place - first_place].append(step)

    for i in range(UNITS * n_sub):
        for m in range(2 * (i % n_sub), 2 * (i % n_sub) + 2):
            put(i, "exp_scores", i // n_sub, m // 4, m % 4)
    for u in range(UNITS):
        start = (u - 1) * n_sub + MAX_LATE
        for m in range(TILES):
            put(start + m // 2, "max_scores", u, m // TT, m % TT)
        for half in range(2):
            put(start + n_sub // 2 * (half + 1) - 1, "max_parts", u, half)
            put(start + n_sub // 2 * (half + 1) + (1, 4)[half], "max_rows", u, half)
        for s in range(n_sub // 2):
            late = u * n_sub + min(2 * s + 2, n_sub - 1)
            put(late, "weigh_v", u, s)
            if s % TT == TT - 1:
                put(late, "heads_evacuate", u, s // TT)
    for t in range(-2, UNITS + 1):
        side = []
        if 0 <= t - 1:
            side += post_steps(t - 1)
        if t + 2 < UNITS:
            side += prep_steps(t + 2)
        for place, step in side:
            put(t * n_sub + place, *step)
    order = [step for place in places for step in place]
    banks = Banks()
    out = []
    for step in order:
        name, u = step[0], step[1]
        if name in TWO_BANKS or (name == "qk_project" and is_ffn(u)):
            use = banks.two()
        elif name in ONE_BANK or name == "qk_project":
            use = banks.one()
        else:
            use = []
        out.append((name, u, step[2:], use))
    return out


def macaron(nc, x, w, out):
    steps = plan()
    with ExitStack() as ctx:
        def sb(name, shape, dt=F32):
            return ctx.enter_context(nc.sbuf_tensor(name, shape, dt))

        def sem(name):
            return ctx.enter_context(nc.semaphore(name))

        X = sb("X", [128, B, TT, C])
        src = sb("src", [128, B, TT, C])
        xT = sb("xT", [128, S])
        rope_c = sb("rope_c", [128, S])
        rope_s = sb("rope_s", [128, S])
        qf = sb("qf", [128, S])
        rest = rope_c
        parts = sb("parts", [128, 2, PARTS, S], BF16)
        q_aug = sb("q_aug", [128, AUG_RING, H, S], BF16)
        k_aug = sb("k_aug", [128, AUG_RING, H, S], BF16)
        v_aug = sb("v_aug", [128, AUG_RING, TT, H * VW])
        maxes = sb("maxes", [128, 2, 2, TT, HH])
        max_rest = sb("max_rest", [128, TT, HH])
        max_parts = sb("max_parts", [128, TT, PARTS, HH], BF16)
        maxT = sb("maxT", [PARTS * HH, S], BF16)
        probs = sb("probs", [128, P_RING, 4, S])
        heads = sb("heads", [128, G4, S])
        denom = sb("denom", [128, TT, H])
        attn = sb("attn", [128, TT, C])
        attnT = sb("attnT", [128, S])
        squares = sb("squares", [128, TT, C], BF16)
        sums = sb("sums", [128, 2, TT])
        mean_var = sb("mean_var", [128, TT, 2])
        stats = sb("stats", [128, TT, 6])
        var_eps = sb("var_eps", [128, TT])
        rstd = sb("rstd", [128, TT])
        rms = sb("rms", [128, 2, TT])
        rms_in = sb("rms_in", [128, TT])
        x1T = sb("x1T", [128, S])
        tanh = sb("tanh", [128, S])
        hidden = sb("hidden", [128, 4, S])
        prod = sb("prod", [128, 2, EPG, C])
        logit = sb("logit", [128, TT, E_GRP + E])
        g_diff = sb("g_diff", [128, TT, 1])
        second = sb("second", [128, TT, 1])
        first = sb("first", [128, TT, 1])
        g_sign = sb("g_sign", [128, TT, 1])
        e_in = sb("e_in", [128, TT, EPG])
        e_tmp = sb("e_tmp", [128, TT, EPG])
        e_max = sb("e_max", [128, TT, 1])
        z = sb("z", [128, TT, EPG + 1])
        ez = sb("ez", [128, TT, EPG + 1])
        e_sum = sb("e_sum", [128, TT, 1])
        g_den = sb("g_den", [128, TT, 1])
        e_den = sb("e_den", [128, TT, 1])
        e_rden = sb("e_rden", [128, TT, 1])
        beaten = sb("beaten", [128, TT, EPG])
        above = sb("above", [128, TT, EPG])
        e_w = sb("e_w", [128, TT, EPG])
        gate = sb("gate", [128, TT, E])
        wq = sb("wq", [128, 2, C])
        wk = sb("wk", [128, 2, C])
        wv = sb("wv", [128, C])
        wo = sb("wo", [128, C])
        kcT = probs[0:DC, 0, 0, 0:2 * C].rearrange("p (i c) -> p i c", i=2)
        kv2 = probs[0:DC, 0, 1, 0:2 * C].rearrange("p (i c) -> p i c", i=2)
        awq = sb("awq", [C // 2, 3, C // 2])
        awo = sb("awo", [C // 2, C])
        w_in = sb("w_in", [128, 2, 2 * HID])
        w_out = sb("w_out", [128, 2, C])
        w2 = sb("w2", [128, 2, E, C])
        w_gate = sb("w_gate", [128, E_GRP + E])
        b_gate = sb("b_gate", [128, 1, E_GRP + E])
        bo = sb("bo", [128, 1, C])
        n1 = sb("n1", [128, C])
        n2 = sb("n2", [128, C])
        cosT = sb("cosT", [128, S])
        sinT = sb("sinT", [128, S])
        ident = sb("ident", [128, 128])
        identb = sb("identb", [128, 128], BF16)
        power = sb("power", [128, TT])
        ones_row = sb("ones_row", [PARTS, 1, S], BF16)
        order0 = sb("order0", [128, TT, EPG])

        ps_max = ctx.enter_context(nc.psum_tensor("ps_max", [128, MAX_RING, S], F32))
        ps_exp = ctx.enter_context(nc.psum_tensor("ps_exp", [128, EXP_RING, S], F32))
        ps_out = ctx.enter_context(nc.psum_tensor("ps_out", [128, S], F32))
        ps = ctx.enter_context(nc.psum_tensor("ps", [128, 2, S], F32))

        scratch = nc.dram_tensor("qk_parts", [2, 2, PARTS, C, S], BF16, kind="Internal").ap()
        scratch_max = nc.dram_tensor("max_parts_rows", [2, PARTS, HH, S], BF16, kind="Internal").ap()

        early_loaded = sem("early_loaded")
        late_loaded = sem("late_loaded")
        x_loaded = sem("x_loaded")
        fused_done = sem("fused_done")
        fused_copied = sem("fused_copied")
        ones_set = sem("ones_set")
        q_cleared = sem("q_cleared")
        k_cleared = sem("k_cleared")
        pool_seq = sem("pool_seq")
        dve_seq = sem("dve_seq")
        bank_full = [sem("bank_full0"), sem("bank_full1")]
        bank_free = [sem("bank_free0"), sem("bank_free1")]
        stats_done = sem("stats_done")
        rstd_done = sem("rstd_done")
        src_done = sem("src_done")
        part_done = sem("part_done")
        parts_stored = [sem("q_parts_stored"), sem("k_parts_stored")]
        aug_loaded = [sem(f"aug_loaded{i}") for i in range(AUG_RING)]
        max_full = sem("max_full")
        max_done = sem("max_done")
        max_split = sem("max_split")
        maxT_stored = sem("maxT_stored")
        max_loaded = [sem("max_loaded0"), sem("max_loaded1")]
        exp_full = sem("exp_full")
        exp_done = sem("exp_done")
        out_done = sem("out_done")
        heads_done = sem("heads_done")
        sums_done = sem("sums_done")
        rms_done = sem("rms_done")
        x1_done = sem("x1_done")
        router_pool = sem("router_pool")
        router_dve = sem("router_dve")
        router_act = sem("router_act")
        tanh_done = sem("tanh_done")
        expert_added = sem("expert_added")
        norm_done = sem("norm_done")
        x_done = sem("x_done")
        stored = sem("stored")

        early = [
            (X[:, 0, :, :], x[0].rearrange("(t p) c -> p t c", p=128)),
            (kcT[:, 0, :], w["ffn_Wk_cT"]), (kcT[:, 1, :], w["ffn_Wv_cT"]),
            (kv2[:, 0, :], w["ffn_Wk"]), (kv2[:, 1, :], w["ffn_Wv"]),
            (ident[:, :], w["ident"]), (wq[:, 0, :], w["ffn_Wq"]),
            (cosT[:, :], w["cosT"]), (sinT[:, :], w["sinT"]),
        ]
        late = [
            (wo[:, :], w["ffn_Wo"]),
            (awq[:, 0, :], w["attn_WqT"]), (awq[:, 1, :], w["attn_WkT"]), (awq[:, 2, :], w["attn_WvT"]),
            (awo[:, :], w["attn_WoT"]),
            (w_in[:, 0, :], w["ffn_W_shared_in"]), (w_in[:, 1, :], w["ffn_W1_shared"]),
            (w_out[:, :, :], w["ffn_W_shared_out"].rearrange("(k p) n -> p k n", p=128)),
            (w2[:, 0, :, :], w["ffn_W2_experts"][:, 0:128, :].rearrange("e p n -> p e n")),
            (w2[:, 1, :, :], w["ffn_W2_experts"][:, 128:256, :].rearrange("e p n -> p e n")),
            (w_gate[:, 0:E_GRP], w["ffn_Wg_gate"]), (w_gate[:, E_GRP:], w["ffn_We_gate"]),
            (b_gate[:, 0, 0:E_GRP], w["ffn_group_bias"].partition_broadcast(128)),
            (b_gate[:, 0, E_GRP:], w["ffn_expert_bias"].partition_broadcast(128)),
            (bo[:, 0, :], w["attn_bo"].partition_broadcast(128)),
            (n1[:, :], w["ffn_norm1_w"].partition_broadcast(128)),
            (n2[:, :], w["ffn_norm2_w"].partition_broadcast(128)),
        ]
        EARLY, LATE = 16 * len(early), 16 * len(late)
        scale = float(np.float32(1) / np.sqrt(np.float32(C // H)))

        uses = {(name, u, *args): use for name, u, args, use in steps}

        def pe_done(engine, *step):
            i, n = uses[step][-1]
            engine.wait_ge(bank_full[i], n + 1)

        def stacked(engine, u):
            engine.wait_ge(aug_loaded[u % AUG_RING], 16 * sum(stack_dmas(v) for v in range(u % AUG_RING, u + 1, AUG_RING)))

        def taken(engine, *step):
            for i, n in uses[step]:
                engine.wait_ge(bank_free[i], n + 1)

        block = ctx.enter_context(nc.Block())

        @block.sync
        def _(sp):
            for to, of in early:
                sp.dma_start(to, of).then_inc(early_loaded, 16)
            for b in range(1, B):
                sp.dma_start(X[:, b, :, :], x[b].rearrange("(t p) c -> p t c", p=128)).then_inc(x_loaded, 16)
            for to, of in late:
                sp.dma_start(to, of).then_inc(late_loaded, 16)
            for name, u, args, use in steps:
                d, r, f = head_dim(u), u % AUG_RING, ffn_index(u)
                rows = H * d
                if name == "qk_split":
                    qk, = args
                    if u >= 2 and qk == 0:
                        stacked(sp, u - 2)
                    sp.wait_ge(part_done, PARTS * (2 * u + qk + 1))
                    sp.dma_start(scratch[u % 2, qk, :, 0:rows, :].rearrange("c p n -> p c n"),
                                 parts[0:rows, qk, :, :]).then_inc(parts_stored[qk], 16)
                elif name == "stack":
                    for of_one in parts_stored:
                        sp.wait_ge(of_one, 16 * (u + 1))
                    if u < 2:
                        sp.wait_ge(q_cleared, u + 1)
                        sp.wait_ge(k_cleared, u + 1)
                    if u >= AUG_RING:
                        sp.wait_ge(exp_full, TILES * (u - AUG_RING + 1))
                    for qk, aug in enumerate((q_aug, k_aug)):
                        v = scratch[u % 2, qk, :, 0:rows, :].rearrange("c (h d) n -> c d h n", d=d)
                        for s in range(PARTS * PARTS):
                            part = s % PARTS if qk else s // PARTS
                            sp.dma_start(aug[d * s:d * s + d, r, :, :], v[part]).then_inc(aug_loaded[r], 16)
                    p0 = product_rows(u)
                    sp.dma_start(k_aug[p0:p0 + PARTS, r, :, :], ones_row[:, :, :].to_broadcast([PARTS, H, S]))\
                        .then_inc(aug_loaded[r], 16)
                    if p0 < product_rows(0):
                        n = product_rows(0) - p0
                        sp.dma_start(k_aug[p0 + PARTS:p0 + PARTS + n, r, :, :],
                                     k_aug[128 - n:128, r, :, :]).then_inc(aug_loaded[r], 16)
                elif name == "max_rows":
                    half, = args
                    taken(sp, "max_rows", u, half)
                    if u:
                        sp.wait_ge(max_loaded[half], 16 * u)
                    sp.dma_start(scratch_max[half].rearrange("c h n -> (c h) n"), maxT[:, :]).then_inc(maxT_stored, 16)
                    sp.wait_ge(maxT_stored, 16 * (2 * u + half + 1))
                    p0 = product_rows(u)
                    sp.dma_start(q_aug[p0:p0 + PARTS, r, half * HH:(half + 1) * HH, :],
                                 scratch_max[half]).then_inc(max_loaded[half], 16)
                elif name == "unit_out" and u // B == LAYERS - 1:
                    b = u % B
                    sp.wait_ge(x_done, u + 1)
                    sp.dma_start(out[b].rearrange("(t p) c -> p t c", p=128), X[:, b, :, :]).then_inc(stored, 16)
            sp.wait_ge(stored, 16 * B)

        @block.tensor
        def _(pe):
            def bank(use):
                i, n = use
                if n:
                    pe.wait_ge(bank_free[i], n)
                return ps[:, i, :]

            pe.wait_ge(early_loaded, EARLY)
            for i in range(2):
                pe.matmul(ps_out[:, i * C:(i + 1) * C], kcT[:, i, :], kv2[:, i, :], start=True, stop=True).then_inc(fused_done, 1)
            for name, u, args, use in steps:
                d, r, b, f, ffn = head_dim(u), u % AUG_RING, u % B, ffn_index(u), is_ffn(u)
                rows = H * d
                if name == "x_transpose":
                    pe.wait_ge(src_done, u + 1)
                    o = bank(use[0])
                    for t in range(TT):
                        mm = pe.transpose(o[0:rows, t * 128:(t + 1) * 128], src[:, b, t, 0:rows], ident[:, :])
                    mm.then_inc(bank_full[use[0][0]], 1)
                elif name == "qk_project":
                    qk, = args
                    taken(pe, "x_transpose", u)
                    if u == 0 and qk == 0:
                        pe.wait_ge(fused_copied, 1)
                    if ffn:
                        for i in range(2):
                            o = bank(use[i])
                            pe.matmul(o, (wq, wk)[qk][:, i, :], xT[:, :], start=True, stop=True)\
                              .then_inc(bank_full[use[i][0]], 1)
                    else:
                        pe.matmul(bank(use[0])[0:rows, :], awq[:, qk, :], xT[0:rows, :], start=True, stop=True)\
                          .then_inc(bank_full[use[0][0]], 1)
                elif name == "v_project":
                    taken(pe, "x_transpose", u)
                    o = bank(use[0])
                    wv_ = wv[:, :] if ffn else awq[:, 2, :]
                    for t in range(TT):
                        mm = pe.matmul(o[:, t * rows:(t + 1) * rows], xT[0:rows, t * 128:(t + 1) * 128], wv_,
                                       start=True, stop=True)
                    mm.then_inc(bank_full[use[0][0]], 1)
                elif name == "max_scores":
                    h, qt = args
                    n, k = u * TILES + h * TT + qt, product_rows(u)
                    if h == 0 and qt == 0:
                        stacked(pe, u)
                    if n >= MAX_RING:
                        pe.wait_ge(max_done, n - MAX_RING + 1)
                    pe.matmul(ps_max[:, n % MAX_RING, :], q_aug[0:k, r, h, qt * 128:(qt + 1) * 128],
                              k_aug[0:k, r, h, :], start=True, stop=True).then_inc(max_full, 1)
                elif name == "max_rows":
                    half, = args
                    pe.wait_ge(max_split, 2 * u + half + 1)
                    o = bank(use[0]).bitcast(BF16)
                    for t in range(TT):
                        mm = pe.transpose(o[0:PARTS * HH, t * 128:(t + 1) * 128],
                                          max_parts[:, t, :, :].rearrange("p c h -> p (c h)"), identb[:, :])
                    mm.then_inc(bank_full[use[0][0]], 1)
                elif name == "exp_scores":
                    s, c = args
                    kt, h = s % TT, 4 * (s // TT) + c
                    n = u * TILES + 4 * s + c
                    if h % HH == 0 and kt == 0:
                        pe.wait_ge(max_loaded[h // HH], 16 * (u + 1))
                    if n >= EXP_RING:
                        pe.wait_ge(exp_done, n - EXP_RING + 1)
                    pe.matmul(ps_exp[:, n % EXP_RING, :], k_aug[:, r, h, kt * 128:(kt + 1) * 128],
                              q_aug[:, r, h, :], start=True, stop=True).then_inc(exp_full, 1)
                elif name == "weigh_v":
                    s, = args
                    g, kt, n = s // TT, s % TT, u * 16 + s
                    pe.wait_ge(exp_done, 4 * (n + 1))
                    if s == 0:
                        taken(pe, "v_project", u)
                    if kt == 0 and u * G4 + g:
                        pe.wait_ge(heads_done, u * G4 + g)
                    for c in range(4):
                        h = 4 * g + c
                        mm = pe.matmul(ps_out[COL * c:COL * c + VW, :], v_aug[:, r, kt, h * VW:(h + 1) * VW],
                                       probs[:, n % P_RING, c, :], start=(kt == 0), stop=(kt == TT - 1))
                    mm.then_inc(out_done, 1)
                elif name == "heads_out":
                    t, = args
                    if t == 0:
                        pe.wait_ge(heads_done, G4 * (u + 1))
                    if u == 0 and t == 0:
                        pe.wait_ge(late_loaded, LATE)
                    o = bank(use[0])
                    for g in range(G4):
                        mm = pe.transpose(o[:, g * 128:(g + 1) * 128], heads[:, g, t * 128:(t + 1) * 128], ident[:, :])
                    mm.then_inc(bank_full[use[0][0]], 1)
                elif name == "heads_transpose":
                    taken(pe, "heads_out", u, TT - 1)
                    o = bank(use[0])
                    for t in range(TT):
                        mm = pe.transpose(o[0:rows, t * 128:(t + 1) * 128], attn[:, t, 0:rows], ident[:, :])
                    mm.then_inc(bank_full[use[0][0]], 1)
                elif name == "out_project":
                    taken(pe, "heads_transpose", u)
                    o = bank(use[0])
                    for t in range(TT):
                        mm = pe.matmul(o[:, t * C:(t + 1) * C], attnT[0:rows, t * 128:(t + 1) * 128],
                                       wo[:, :] if ffn else awo[:, :], start=True, stop=True)
                    mm.then_inc(bank_full[use[0][0]], 1)
                elif name == "x1_transpose":
                    pe.wait_ge(x1_done, f + 1)
                    o = bank(use[0])
                    for t in range(TT):
                        mm = pe.transpose(o[:, t * 128:(t + 1) * 128], src[:, b, t, :], ident[:, :])
                    mm.then_inc(bank_full[use[0][0]], 1)
                elif name == "logits":
                    taken(pe, "x1_transpose", u)
                    o, n = bank(use[0]), E_GRP + E
                    for t in range(TT):
                        mm = pe.matmul(o[:, t * n:(t + 1) * n], x1T[:, t * 128:(t + 1) * 128], w_gate[:, :],
                                       start=True, stop=True)
                    mm.then_inc(bank_full[use[0][0]], 1)
                elif name == "mlp_up":
                    c, = args
                    taken(pe, "x1_transpose", u)
                    for i in range(2):
                        c0 = i * HID + (c % 2) * 128
                        pe.matmul(bank(use[i]), w_in[:, c // 2, c0:c0 + 128], x1T[:, :], start=True, stop=True)\
                          .then_inc(bank_full[use[i][0]], 1)
                elif name == "shared_out":
                    taken(pe, "mlp_up", u, 1)
                    o = bank(use[0])
                    for t in range(TT):
                        for k in range(2):
                            mm = pe.matmul(o[:, t * C:(t + 1) * C], hidden[:, k, t * 128:(t + 1) * 128],
                                           w_out[:, k, :], start=(k == 0), stop=(k == 1))
                    mm.then_inc(bank_full[use[0][0]], 1)
                elif name == "expert":
                    t, half = args
                    taken(pe, "mlp_up", u, 3)
                    o = bank(use[0])
                    for k in range(2):
                        mm = pe.matmul(o, hidden[:, 2 + k, t * 128:(t + 1) * 128],
                                       w2[:, k, half * EPG:(half + 1) * EPG, :].rearrange("p e n -> p (e n)"),
                                       start=(k == 0), stop=(k == 1))
                    mm.then_inc(bank_full[use[0][0]], 1)

        @block.vector
        def _(dve):
            own = [0]

            def seq(ins):
                own[0] += 1
                ins.then_inc(dve_seq, 1)

            def own_wait():
                dve.wait_ge(dve_seq, own[0])

            def full(use):
                i, n = use
                dve.wait_ge(bank_full[i], n + 1)
                return ps[:, i, :]

            dve.memset(q_aug[64:128, 0, :, :].bitcast(F32), 0.0).then_inc(q_cleared, 1)
            dve.wait_ge(early_loaded, EARLY)
            for name, u, args, use in steps:
                d, r, b, f, ffn = head_dim(u), u % AUG_RING, u % B, ffn_index(u), is_ffn(u)
                rows = H * d
                if name == "norm_stats":
                    if u >= B:
                        dve.wait_ge(x_done, u - B + 1)
                    if u == 1:
                        dve.wait_ge(x_loaded, 16 * (B - 1))
                    if u:
                        dve.wait_ge(src_done, u)
                    for t in range(TT):
                        seq(dve.bn_stats(stats[:, t, :], X[:, b, t, :]))
                    own_wait()
                    for t in range(TT):
                        ins = dve.bn_aggr(mean_var[:, t, :], stats[:, t, :])
                        if t < TT - 1:
                            seq(ins)
                    ins.then_inc(stats_done, 1)
                elif name == "norm_apply":
                    if u == 0:
                        dve.wait_ge(fused_done, 2)
                        seq(dve.tensor_copy(wk[:, 0, :], ps_out[:, 0:C]))
                        own_wait()
                        for t in (wq, wk):
                            plain = t[:, 0, :].rearrange("p (i e) -> p i e", e=2)
                            turned = t[:, 1, :].rearrange("p (i e) -> p i e", e=2)
                            seq(dve.tensor_scalar(turned[:, :, 0], plain[:, :, 1], -1.0, None, ALU.mult))
                            seq(dve.tensor_copy(turned[:, :, 1], plain[:, :, 0]))
                        seq(dve.tensor_copy(identb[:, :], ident[:, :]))
                        seq(dve.tensor_copy(wv[:, :], ps_out[:, C:2 * C]))
                        own_wait()
                        dve.memset(ps_out[:, :], 0.0).then_inc(fused_copied, 1)
                    dve.wait_ge(rstd_done, u + 1)
                    own_wait()
                    dve.wait_ge(stats_done, u + 1)
                    for t in range(TT):
                        ins = dve.tensor_scalar(src[:, b, t, :], X[:, b, t, :], mean_var[:, t, 0:1], rstd[:, t:t + 1],
                                                ALU.subtract, ALU.mult)
                    ins.then_inc(src_done, 1)
                elif name == "qk_project" and ffn:
                    qk, = args
                    if u + qk:
                        dve.wait_ge(part_done, PARTS * (2 * u + qk))
                    dve.tensor_tensor(rope_c[:, :], full(use[0]), cosT[:, :], ALU.mult).then_inc(bank_free[use[0][0]], 1)
                    ins = dve.tensor_tensor(rope_s[:, :], full(use[1]), sinT[:, :], ALU.mult)
                    ins.then_inc(bank_free[use[1][0]], 1)
                    if u == 0 and qk == 1:
                        dve.memset(q_aug[64:128, 1:, :, :].bitcast(F32), 0.0).then_inc(q_cleared, 1)
                elif name == "max_scores":
                    h, qt = args
                    n = u * TILES + h * TT + qt
                    if h == 0 and qt == 0 and u >= 2:
                        dve.wait_ge(max_split, 2 * (u - 1))
                    dve.wait_ge(max_full, n + 1)
                    dve.tensor_reduce(maxes[:, u % 2, h // HH, qt, h % HH:h % HH + 1], ps_max[:, n % MAX_RING, :],
                                      AX.X, ALU.max).then_inc(max_done, 1)
                elif name == "heads_out":
                    t, = args
                    if u == 0 and t == 0:
                        dve.wait_ge(late_loaded, LATE)
                        seq(dve.tensor_scalar(n2[:, :], n2[:, :], 0.5, None, ALU.mult))
                    tile = full(use[0]).rearrange("p (h e) -> p h e", e=COL)
                    seq(dve.reciprocal(denom[:, t, :].unsqueeze(2), tile[:, :, ONE_COL:ONE_COL + 1]))
                    own_wait()
                    if u and t == 0:
                        taken(dve, "heads_transpose", u - 1)
                    ins = dve.tensor_tensor(attn[:, t, 0:rows].rearrange("p (h e) -> p h e", e=d), tile[:, :, 0:d],
                                            denom[:, t, :].unsqueeze(2).to_broadcast([128, H, d]), ALU.mult)
                    ins.then_inc(bank_free[use[0][0]], 1)
                elif name == "out_project":
                    o = full(use[0]).rearrange("p (t c) -> p t c", c=C)
                    if ffn:
                        ins = dve.tensor_tensor(src[:, b, :, :], o, src[:, b, :, :], ALU.add)
                        ins.then_inc(bank_free[use[0][0]], 1)
                    else:
                        ins = dve.tensor_tensor(X[:, b, :, :], o, X[:, b, :, :], ALU.add)
                        ins.then_inc(bank_free[use[0][0]], 1)
                elif name == "rms_apply1":
                    dve.wait_ge(rms_done, 2 * f + 1)
                    taken(dve, "out_project", u)
                    for t in range(TT):
                        ins = dve.scalar_tensor_tensor(out=src[:, b, t, :], in0=src[:, b, t, :], scalar=rms[:, 0, t:t + 1],
                                                       in1=n1[:, :], op0=ALU.mult, op1=ALU.mult)
                    ins.then_inc(x1_done, 1)
                elif name == "logits":
                    if f:
                        dve.wait_ge(router_pool, 4 * f)
                    n = E_GRP + E
                    ins = dve.tensor_tensor(logit[:, :, :], full(use[0])[:, 0:TT * n].rearrange("p (t n) -> p t n", n=n),
                                            b_gate[:, :, :].to_broadcast([128, TT, n]), ALU.add)
                    ins.then_inc(bank_free[use[0][0]], 1)
                elif name == "router":
                    k, = args
                    if k == 1:
                        dve.wait_ge(router_pool, 4 * f + 1)
                        dve.tensor_reduce(e_max[:, :, :], e_in[:, :, :], AX.X, ALU.max).then_inc(router_dve, 1)
                    elif k == 4:
                        dve.wait_ge(router_act, f + 1)
                        dve.tensor_reduce(e_sum[:, :, :], ez[:, :, 0:EPG], AX.X, ALU.add).then_inc(router_dve, 1)
                    elif k == 6:
                        dve.wait_ge(router_pool, 4 * f + 3)
                        dve.reciprocal(e_rden[:, :, :], e_den[:, :, :]).then_inc(router_dve, 1)
                elif name == "mlp_up":
                    c, = args
                    if f:
                        pe_done(dve, *(("shared_out", before(u)) if c < 2 else ("expert", before(u), TT - 1, 1)))
                    dve.wait_ge(tanh_done, 4 * f + c + 1)
                    ins = dve.scalar_tensor_tensor(out=tanh[:, :], in0=tanh[:, :], scalar=1.0, in1=full(use[0]),
                                                   op0=ALU.add, op1=ALU.mult)
                    ins.then_inc(bank_free[use[0][0]], 1)
                    dve.wait_ge(bank_free[use[0][0]], use[0][1] + 1)
                    ins = dve.scalar_tensor_tensor(out=hidden[:, c, :], in0=tanh[:, :], scalar=0.5, in1=full(use[1]),
                                                   op0=ALU.mult, op1=ALU.mult)
                    ins.then_inc(bank_free[use[1][0]], 1)
                elif name == "shared_out":
                    dve.wait_ge(x1_done, f + 1)
                    ins = dve.tensor_tensor(src[:, b, :, :], full(use[0]).rearrange("p (t c) -> p t c", c=C),
                                            src[:, b, :, :], ALU.add)
                    ins.then_inc(bank_free[use[0][0]], 1)
                elif name == "expert":
                    t, half = args
                    n = (f * TT + t) * 2 + half
                    dve.wait_ge(router_pool, 4 * (f + 1))
                    if n >= 2:
                        dve.wait_ge(expert_added, n // 2)
                    ins = dve.tensor_tensor(prod[:, half, :, :], full(use[0]).rearrange("p (e c) -> p e c", c=C),
                                            gate[:, t, half * EPG:(half + 1) * EPG].unsqueeze(2)
                                            .to_broadcast([128, EPG, C]), ALU.mult)
                    ins.then_inc(bank_free[use[0][0]], 1)
                elif name == "rms_apply2":
                    dve.wait_ge(rms_done, 2 * f + 2)
                    dve.wait_ge(expert_added, TT * (f + 1))
                    for t in range(TT):
                        ins = dve.scalar_tensor_tensor(out=src[:, b, t, :], in0=src[:, b, t, :],
                                                       scalar=rms[:, 1, t:t + 1], in1=n2[:, :],
                                                       op0=ALU.mult, op1=ALU.mult)
                    ins.then_inc(norm_done, 1)

        @block.scalar
        def _(act):
            def full(use):
                i, n = use
                act.wait_ge(bank_full[i], n + 1)
                return ps[:, i, :]

            act.wait_ge(ones_set, 1)
            for name, u, args, use in steps:
                d, r, b, f, ffn = head_dim(u), u % AUG_RING, u % B, ffn_index(u), is_ffn(u)
                rows = H * d
                if name == "x_transpose":
                    if u:
                        pe_done(act, "v_project", u - 1)
                    ins = act.activation(xT[0:rows, :], full(use[0])[0:rows, :], ACT.Copy)
                    ins.then_inc(bank_free[use[0][0]], 1)
                elif name == "qk_project" and not ffn:
                    qk, = args
                    act.wait_ge(part_done, PARTS * (2 * u + qk))
                    ins = act.activation(qf[0:rows, :], full(use[0])[0:rows, :], ACT.Copy)
                    ins.then_inc(bank_free[use[0][0]], 1)
                elif name == "v_project":
                    if u >= AUG_RING:
                        act.wait_ge(out_done, 16 * (u - AUG_RING + 1))
                    to = v_aug[:, r, :, :].rearrange("p t (h e) -> p (t h) e", e=VW)[:, :, 0:d]
                    ins = act.activation(to, full(use[0])[:, 0:TT * rows].rearrange("p (m e) -> p m e", e=d), ACT.Copy)
                    ins.then_inc(bank_free[use[0][0]], 1)
                elif name == "max_rows":
                    half, = args
                    if u + half:
                        act.wait_ge(maxT_stored, 16 * (2 * u + half))
                    n = PARTS * HH
                    ins = act.activation(maxT[:, :], full(use[0]).bitcast(BF16)[0:n, 0:S], ACT.Copy)
                    ins.then_inc(bank_free[use[0][0]], 1)
                elif name == "exp_scores":
                    s, c = args
                    n, step = u * TILES + 4 * s + c, u * 16 + s
                    act.wait_ge(exp_full, n + 1)
                    if c == 0 and step >= P_RING:
                        act.wait_ge(out_done, step - P_RING + 1)
                    act.activation(probs[:, step % P_RING, c, :], ps_exp[:, n % EXP_RING, :], ACT.Exp,
                                   scale=scale).then_inc(exp_done, 1)
                elif name == "heads_evacuate":
                    g, = args
                    act.wait_ge(out_done, u * 16 + TT * (g + 1))
                    if u:
                        pe_done(act, "heads_out", u - 1, TT - 1)
                    act.activation(heads[:, g, :], ps_out[:, :], ACT.Copy).then_inc(heads_done, 1)
                elif name == "heads_transpose":
                    if u:
                        pe_done(act, "out_project", u - 1)
                    ins = act.activation(attnT[0:rows, :], full(use[0])[0:rows, :], ACT.Copy)
                    ins.then_inc(bank_free[use[0][0]], 1)
                elif name == "rms_stats":
                    which, = args
                    if which == 0:
                        taken(act, "out_project", u)
                    else:
                        act.wait_ge(expert_added, TT * (f + 1))
                    if f + which:
                        act.wait_ge(sums_done, 2 * f + which)
                    if f:
                        act.wait_ge(rms_done, 2 * f - 1 + which)
                    for t in range(TT):
                        ins = act.activation(squares[:, t, :], src[:, b, t, :], ACT.Square, accum_out=sums[:, which, t:t + 1])
                    ins.then_inc(sums_done, 1)
                elif name == "x1_transpose":
                    if f:
                        pe_done(act, "mlp_up", before(u), 3)
                    ins = act.activation(x1T[:, :], full(use[0]), ACT.Copy)
                    ins.then_inc(bank_free[use[0][0]], 1)
                elif name == "router" and args[0] == 3:
                    act.wait_ge(router_pool, 4 * f + 2)
                    act.activation(ez[:, :, :], z[:, :, :], ACT.Exp).then_inc(router_act, 1)
                elif name == "mlp_up":
                    c, = args
                    if f + c:
                        taken(act, "mlp_up", u if c else before(u), (c - 1) % 4)
                    act.activation(tanh[:, :], full(use[0]), ACT.Tanh, scale=0.5).then_inc(tanh_done, 1)

        @block.gpsimd
        def _(pool):
            own = [0]

            def seq(ins):
                own[0] += 1
                ins.then_inc(pool_seq, 1)
                return ins

            def own_wait():
                pool.wait_ge(pool_seq, own[0])

            seq(pool.memset(v_aug[:, :, :, :], 0.0))
            own_wait()
            seq(pool.memset(power[:, :], -0.5))
            seq(pool.memset(ones_row[:, :, :], 1.0))
            for e in range(EPG):
                seq(pool.memset(order0[:, :, e:e + 1], float(e)))
            own_wait()
            ones = v_aug[:, :, :, :].rearrange("p r t (h e) -> p (r t h) e", e=VW)[:, :, ONE_COL:ONE_COL + 1]
            pool.memset(ones, 1.0).then_inc(ones_set, 1)
            pool.wait_ge(ones_set, 1)
            pool.memset(k_aug[64:128, 0, :, :].bitcast(F32), 0.0).then_inc(k_cleared, 1)
            pool.wait_ge(k_cleared, 1)
            for name, u, args, use in steps:
                d, r, b, f, ffn = head_dim(u), u % AUG_RING, u % B, ffn_index(u), is_ffn(u)
                rows = H * d
                if name == "norm_stats":
                    pool.wait_ge(stats_done, u + 1)
                    seq(pool.tensor_scalar(var_eps[:, :].unsqueeze(2), mean_var[:, :, 1:2], LN_EPS, None, ALU.add))
                    own_wait()
                    if u:
                        pool.wait_ge(src_done, u)
                    pool.tensor_tensor(rstd[:, :], var_eps[:, :], power[:, :], ALU.pow).then_inc(rstd_done, 1)
                elif name == "qk_split":
                    qk, = args
                    q = qf[0:rows, :]
                    if ffn:
                        taken(pool, "qk_project", u, qk)
                        if u + qk:
                            pool.wait_ge(part_done, PARTS * (2 * u + qk))
                        ins = pool.tensor_tensor(q, rope_c[:, :], rope_s[:, :], ALU.add)
                        seq(ins)
                        own_wait()
                    else:
                        taken(pool, "qk_project", u, qk)
                    if u:
                        pool.wait_ge(parts_stored[qk], 16 * u)
                    h, m, l = (parts[0:rows, qk, c, :] for c in range(PARTS))
                    n = PARTS * (2 * u + qk)
                    pool.tensor_copy(h, q).then_inc(part_done, 1)
                    pool.wait_ge(part_done, n + 1)
                    seq(pool.tensor_tensor(rest[0:rows, :], q, h, ALU.subtract))
                    own_wait()
                    pool.tensor_copy(m, rest[0:rows, :]).then_inc(part_done, 1)
                    pool.wait_ge(part_done, n + 2)
                    pool.tensor_tensor(l, rest[0:rows, :], m, ALU.subtract).then_inc(part_done, 1)
                    if u == 0 and qk == 1:
                        pool.wait_ge(part_done, n + 3)
                        pool.memset(k_aug[64:128, 1:, :, :].bitcast(F32), 0.0).then_inc(k_cleared, 1)
                        pool.wait_ge(k_cleared, 2)
                elif name == "max_parts":
                    half, = args
                    pool.wait_ge(max_done, u * TILES + TILES // 2 * (half + 1))
                    if u + half:
                        pe_done(pool, "max_rows", *((u, 0) if half else (u - 1, 1)))
                    mx = maxes[:, u % 2, half, :, :]
                    h, m, l = (max_parts[:, :, c, :] for c in range(PARTS))
                    seq(pool.tensor_scalar(h, mx, -1.0, None, ALU.mult))
                    own_wait()
                    seq(pool.tensor_tensor(max_rest[:, :, :], mx, h, ALU.add))
                    own_wait()
                    seq(pool.tensor_scalar(m, max_rest[:, :, :], -1.0, None, ALU.mult))
                    own_wait()
                    seq(pool.tensor_tensor(max_rest[:, :, :], max_rest[:, :, :], m, ALU.add))
                    own_wait()
                    pool.tensor_scalar(l, max_rest[:, :, :], -1.0, None, ALU.mult).then_inc(max_split, 1)
                elif name == "rms_stats":
                    which, = args
                    pool.wait_ge(sums_done, 2 * f + which + 1)
                    seq(pool.tensor_scalar(rms_in[:, :], sums[:, which, :], 1.0 / C, RMS_EPS, ALU.mult, ALU.add))
                    own_wait()
                    if f:
                        pool.wait_ge((x1_done, norm_done)[which], f)
                    pool.tensor_tensor(rms[:, which, :], rms_in[:, :], power[:, :], ALU.pow).then_inc(rms_done, 1)
                elif name == "router":
                    k, = args
                    wide = [128, TT, EPG]
                    if k == 0:
                        taken(pool, "logits", u)
                        if f:
                            pool.wait_ge(router_dve, 3 * f)
                        seq(pool.tensor_tensor(g_diff[:, :, :], logit[:, :, 1:2], logit[:, :, 0:1], ALU.subtract))
                        own_wait()
                        seq(pool.tensor_scalar(second[:, :, :], g_diff[:, :, :], 0.0, None, ALU.is_gt))
                        own_wait()
                        seq(pool.tensor_scalar(first[:, :, :], second[:, :, :], -1.0, 1.0, ALU.mult, ALU.add))
                        seq(pool.tensor_tensor(e_tmp[:, :, :], logit[:, :, E_GRP + EPG:], second[:, :, :].to_broadcast(wide),
                                               ALU.mult))
                        own_wait()
                        seq(pool.tensor_tensor(e_in[:, :, :], logit[:, :, E_GRP:E_GRP + EPG],
                                               first[:, :, :].to_broadcast(wide), ALU.mult))
                        own_wait()
                        pool.tensor_tensor(e_in[:, :, :], e_in[:, :, :], e_tmp[:, :, :], ALU.add).then_inc(router_pool, 1)
                    elif k == 2:
                        pool.wait_ge(router_dve, 3 * f + 1)
                        seq(pool.tensor_tensor(z[:, :, 0:EPG], e_in[:, :, :], e_max[:, :, :].to_broadcast(wide),
                                               ALU.subtract))
                        seq(pool.tensor_tensor(g_sign[:, :, :], first[:, :, :], second[:, :, :], ALU.subtract))
                        own_wait()
                        pool.tensor_tensor(z[:, :, EPG:EPG + 1], g_diff[:, :, :], g_sign[:, :, :], ALU.mult)\
                            .then_inc(router_pool, 1)
                        seq(pool.tensor_copy(beaten[:, :, :], order0[:, :, :]))
                        for s in range(1, EPG):
                            lo, hi, n = slice(0, EPG - s), slice(s, EPG), EPG - s
                            seq(pool.tensor_tensor(above[:, :, 0:n], e_in[:, :, hi], e_in[:, :, lo], ALU.subtract))
                            own_wait()
                            seq(pool.tensor_scalar(above[:, :, 0:n], above[:, :, 0:n], 0.0, None, ALU.is_gt))
                            own_wait()
                            seq(pool.tensor_tensor(beaten[:, :, lo], beaten[:, :, lo], above[:, :, 0:n], ALU.add))
                            own_wait()
                            seq(pool.tensor_tensor(beaten[:, :, hi], beaten[:, :, hi], above[:, :, 0:n], ALU.subtract))
                            own_wait()
                        seq(pool.tensor_scalar(beaten[:, :, :], beaten[:, :, :], 1.5, None, ALU.is_lt))
                    elif k == 5:
                        pool.wait_ge(router_dve, 3 * f + 2)
                        seq(pool.tensor_scalar(g_den[:, :, :], ez[:, :, EPG:EPG + 1], 1.0, None, ALU.add))
                        own_wait()
                        pool.tensor_tensor(e_den[:, :, :], e_sum[:, :, :], g_den[:, :, :], ALU.mult)\
                            .then_inc(router_pool, 1)
                        seq(pool.tensor_tensor(e_w[:, :, :], ez[:, :, 0:EPG], beaten[:, :, :], ALU.mult))
                    elif k == 7:
                        pool.wait_ge(router_dve, 3 * f + 3)
                        own_wait()
                        seq(pool.tensor_tensor(e_w[:, :, :], e_w[:, :, :], e_rden[:, :, :].to_broadcast(wide), ALU.mult))
                        own_wait()
                        if f:
                            taken(pool, "expert", before(u), TT - 1, 1)
                        seq(pool.tensor_tensor(gate[:, :, 0:EPG], e_w[:, :, :], first[:, :, :].to_broadcast(wide), ALU.mult))
                        own_wait()
                        pool.tensor_tensor(gate[:, :, EPG:], e_w[:, :, :], second[:, :, :].to_broadcast(wide), ALU.mult)\
                            .then_inc(router_pool, 1)
                elif name == "expert" and args[1] == 1:
                    t = args[0]
                    taken(pool, "expert", u, t, 0)
                    taken(pool, "expert", u, t, 1)
                    if t == 0:
                        taken(pool, "shared_out", u)
                    seq(pool.tensor_tensor(prod[:, 0, :, :], prod[:, 0, :, :], prod[:, 1, :, :], ALU.add))
                    own_wait()
                    seq(pool.tensor_tensor(prod[:, 0, 0:2, :], prod[:, 0, 0:2, :], prod[:, 0, 2:4, :], ALU.add))
                    own_wait()
                    seq(pool.tensor_tensor(src[:, b, t, :], src[:, b, t, :], prod[:, 0, 0, :], ALU.add))
                    own_wait()
                    pool.tensor_tensor(src[:, b, t, :], src[:, b, t, :], prod[:, 0, 1, :], ALU.add).then_inc(expert_added, 1)
                elif name == "unit_out":
                    if ffn:
                        pool.wait_ge(norm_done, f + 1)
                        if u >= B:
                            pool.wait_ge(x_done, u - B + 1)
                        pool.tensor_tensor(X[:, b, :, :], X[:, b, :, :], src[:, b, :, :], ALU.add).then_inc(x_done, 1)
                    else:
                        taken(pool, "out_project", u)
                        if u == B:
                            pool.wait_ge(late_loaded, LATE)
                        pool.tensor_tensor(X[:, b, :, :], X[:, b, :, :], bo[:, :, :].to_broadcast([128, TT, C]), ALU.add)\
                            .then_inc(x_done, 1)


_PLAIN = ["ffn_Wq", "ffn_Wo", "ffn_Wk", "ffn_Wv", "ffn_W_shared_in", "ffn_W1_shared", "ffn_W_shared_out",
          "ffn_W2_experts", "ffn_Wg_gate", "ffn_We_gate", "ffn_group_bias", "ffn_expert_bias", "ffn_norm1_w",
          "ffn_norm2_w", "attn_bo"]
_TURNED = ["ffn_Wk_c", "ffn_Wv_c", "attn_Wq", "attn_Wk", "attn_Wv", "attn_Wo"]


def shape_constants():
    dh = C // H
    inv = (1.0 / np.power(np.float32(10000.0), np.arange(0, dh, 2, dtype=np.float32) / np.float32(dh))).astype(np.float32)
    ang = np.arange(S, dtype=np.float32)[:, None] * inv[None, :]
    rows = (np.arange(C) % dh) // 2
    out = {"cosT": np.cos(ang).T[rows], "sinT": np.sin(ang).T[rows], "ident": np.eye(128)}
    out = {k: np.ascontiguousarray(v, dtype=np.float32) for k, v in out.items()}
    return out


def kernel(**inputs):
    import concourse.bacc as _bacc
    from concourse.bass_utils import run_bass_kernel_spmd as _run

    nc = _bacc.Bacc("TRN2", target_bir_lowering=False, num_devices=1)
    arrays = {"x": np.ascontiguousarray(inputs["L0_attn_x"])}
    for name in _PLAIN:
        arrays[name] = np.ascontiguousarray(inputs["L0_" + name])
    for name in _TURNED:
        arrays[name + "T"] = np.ascontiguousarray(np.transpose(inputs["L0_" + name]))
    arrays.update(shape_constants())
    aps, feed = {}, {}
    for name, a in arrays.items():
        feed[f"in_{name}_dram"] = a
        aps[name] = nc.dram_tensor(f"in_{name}_dram", a.shape, mybir.dt.from_np(a.dtype), kind="ExternalInput").ap()
    out = nc.dram_tensor("out_0_dram", (B, S, C), F32, kind="ExternalOutput").ap()
    macaron(nc, aps.pop("x"), aps, out)
    r = _run(nc, [feed], core_ids=[0])
    return r.results[0]["out_0_dram"]
```

```python
from contextlib import ExitStack

import concourse.bass as bass
from concourse import mybir
import numpy as np

F32 = mybir.dt.float32
BF16 = mybir.dt.bfloat16
ALU = mybir.AluOpType
ACT = mybir.ActivationFunctionType
AX = mybir.AxisListType

B, S, C = 4, 512, 128
TT = S // 128
H = 16
HH = H // 2
G4 = H // 4
LAYERS = 3
UNITS = LAYERS * B
E_GRP, EPG = 2, 4
E = E_GRP * EPG
HID = 256
DC = 32
LN_EPS, RMS_EPS = 1e-5, 1e-6
PARTS = 3
COL = 32
VW = 9
ONE_COL = 8
AUG_RING = 3
MAX_RING, EXP_RING = 3, 2
TILES = H * TT
VECTOR_SPLITS = {0}
VECTOR_EXPERTS = {UNITS - 1}
P_RING = 2


def is_ffn(u):
    return u // B != 1


def ffn_index(u):
    return u if u < B else (B if u < 2 * B else u - B)


def before(u):
    return u - 1 if is_ffn(u - 1) else u - 1 - B


def head_dim(u):
    return C // H if is_ffn(u) else C // 2 // H


def product_rows(u):
    return head_dim(u) * PARTS * PARTS


def stack_dmas(u):
    return 2 * PARTS + 1 + (product_rows(u) < product_rows(0))


class Banks:

    def __init__(self):
        self.uses = [0] * (2 + MAX_RING + EXP_RING)
        self.order = list(range(len(self.uses)))

    def take(self, count, free):
        taken = []
        for _ in range(count):
            bank = next(i for i in self.order if i < free)
            self.order.remove(bank)
            self.order.append(bank)
            self.uses[bank] += 1
            taken.append((bank, self.uses[bank] - 1))
        return taken


PREP = {"norm_stats": [5], "norm_apply": [7], "x_transpose": [10], "qk_project": [14, 26], "qk_split": [19, 27],
        "v_project": [16], "stack": [26, 44]}
PREP_SECOND = {"norm_stats": [0], "norm_apply": [10], "x_transpose": [13], "qk_project": [13, 30],
               "qk_split": [26, 43], "v_project": [27], "stack": [28, 62]}
PREP_ATTN = {"norm_stats": [5], "norm_apply": [7], "x_transpose": [11], "qk_project": [14, 26], "qk_split": [22, 40],
             "v_project": [15], "stack": [26, 56]}
POST = {"heads_out": [1, 3, 4, 5], "heads_transpose": [7], "out_project": [9], "rms_stats": [13, 61],
        "rms_apply1": [16], "x1_transpose": [19], "logits": [26], "mlp_up": [23, 28, 31, 34],
        "router": [26, 27, 27, 30, 35, 35, 37, 38], "shared_out": [38], "expert": [40, 42, 43, 47, 49, 50, 50, 54],
        "rms_apply2": [63], "ffn_out": [63]}
POST_ATTN = {"heads_out": [2, 2, 3, 3], "heads_transpose": [8], "out_project": [10], "attn_out": [12]}
POST_LAST_BUT_ONE = {"heads_out": [3, 3, 5, 5], "heads_transpose": [8], "out_project": [9], "rms_stats": [11, 61],
                     "rms_apply1": [14], "x1_transpose": [18], "logits": [22], "mlp_up": [23, 28, 31, 34],
                     "router": [27, 27, 29, 30, 35, 35, 37, 39], "shared_out": [39],
                     "expert": [45, 47, 49, 51, 52, 54, 56, 56], "rms_apply2": [61], "ffn_out": [61]}
POST_LAST = {"heads_out": [3, 3, 4, 4], "heads_transpose": [7], "out_project": [8], "rms_stats": [10],
             "rms_apply1": [10], "x1_transpose": [13], "logits": [15], "mlp_up": [14, 18, 23, 27],
             "router": [17, 18, 18, 24, 26, 26, 28, 30], "shared_out": [28],
             "expert": [36, 36, 37, 42, 43, 43, 48, 52]}
MAX_LATE = 15
ROWS_LATE = [5, 5]
WEIGH_LATE = 2


def prep_steps(u):
    at = PREP_SECOND if u == 1 else PREP if is_ffn(u) else PREP_ATTN
    steps = [(at[name][0], (name, u)) for name in ("norm_stats", "norm_apply", "x_transpose")]
    steps += [(at["qk_project"][0], ("qk_project", u, 0)), (at["qk_split"][0], ("qk_split", u, 0)),
              (at["v_project"][0], ("v_project", u)),
              (at["qk_project"][1], ("qk_project", u, 1)), (at["qk_split"][1], ("qk_split", u, 1))]
    return steps + [(at["stack"][qk], ("stack", u, qk)) for qk in range(2)]


def post_steps(u):
    at = POST_LAST if u == UNITS - 1 else POST_LAST_BUT_ONE if u == UNITS - 2 else POST if is_ffn(u) else POST_ATTN

    def several(name):
        return [(place, (name, u, i)) for i, place in enumerate(at[name])]

    steps = several("heads_out") + [(at[name][0], (name, u)) for name in ("heads_transpose", "out_project")]
    if not is_ffn(u):
        return steps + [(at["attn_out"][0], ("unit_out", u))]
    stats = several("rms_stats")
    steps += stats[:1] + [(at[name][0], (name, u)) for name in ("rms_apply1", "x1_transpose", "logits")]
    steps += several("mlp_up") + several("router") + [(at["shared_out"][0], ("shared_out", u))]
    steps += [(place, ("expert", u, i // 2, i % 2)) for i, place in enumerate(at["expert"])]
    if u == UNITS - 1:
        last = [at["expert"][2 * min(t + 1, TT - 1) + 1] for t in range(TT)]
        return steps + [(place, ("finish", u, t)) for t, place in enumerate(last)]
    return steps + stats[1:] + [(at["rms_apply2"][0], ("rms_apply2", u)), (at["ffn_out"][0], ("unit_out", u))]


ONE_BANK = {"x_transpose", "qk_project", "v_project", "heads_transpose", "out_project", "x1_transpose", "logits", "shared_out",
            "expert", "max_rows", "heads_out"}
TWO_BANKS = {"mlp_up"}


def plan():
    order = []
    first_place = -2 * TILES
    places = [[] for _ in range((UNITS + 5) * TILES)]

    def put(place, *step):
        places[place - first_place].append(step)

    for i in range(UNITS * TILES):
        put(i, "exp_scores", i // TILES, i % TILES // 4, i % 4)
    for u in range(UNITS):
        start = (u - 1) * TILES + MAX_LATE
        for m in range(TILES):
            put(start + m, "max_scores", u, m // TT, m % TT)
        for half in range(2):
            end = start + TILES // 2 * (half + 1) - 1
            put(end, "max_parts", u, half)
            put(end + ROWS_LATE[half], "max_rows", u, half)
        for s in range(TILES // 4):
            late = u * TILES + 4 * s + 3 + WEIGH_LATE
            put(late, "weigh_v", u, s)
            if s % TT == TT - 1:
                put(late, "heads_evacuate", u, s // TT)
    for t in range(-2, UNITS + 1):
        side = []
        if 0 <= t - 1:
            side += post_steps(t - 1)
        if t + 2 < UNITS:
            side += prep_steps(t + 2)
        for place, step in side:
            put(t * TILES + place, *step)
    banks = Banks()
    out = []
    max_end = (UNITS - 1) * TILES + MAX_LATE
    exp_end = UNITS * TILES
    for place, steps in enumerate(places, first_place):
        free = 2 + MAX_RING * (place >= max_end) + EXP_RING * (place >= exp_end)
        for step in steps:
            name, u = step[0], step[1]
            use = banks.take(2 if name in TWO_BANKS else 1 if name in ONE_BANK else 0, free)
            out.append((name, u, step[2:], use))
    return out


def macaron(nc, x, w, out):
    steps = plan()
    with ExitStack() as ctx:
        def sb(name, shape, dt=F32):
            return ctx.enter_context(nc.sbuf_tensor(name, shape, dt))

        def sem(name):
            return ctx.enter_context(nc.semaphore(name))

        X = sb("X", [128, B, TT, C])
        src = sb("src", [128, B, TT, C])
        xT = sb("xT", [128, S])
        rope_c = sb("rope_c", [128, S])
        rope_s = sb("rope_s", [128, S])
        qf = sb("qf", [128, S])
        rest = rope_c
        parts = sb("parts", [128, 2, PARTS, S], BF16)
        q_aug = sb("q_aug", [128, AUG_RING, H, S], BF16)
        k_aug = sb("k_aug", [128, AUG_RING, H, S], BF16)
        v_aug = sb("v_aug", [128, AUG_RING, TT, H * VW])
        maxes = sb("maxes", [128, 2, 2, TT, HH])
        max_rest = sb("max_rest", [128, TT, HH])
        max_parts = sb("max_parts", [128, TT, PARTS, HH], BF16)
        maxT = sb("maxT", [PARTS * HH, S], BF16)
        probs = sb("probs", [128, P_RING, 4, S])
        heads = sb("heads", [128, G4, S])
        denom = sb("denom", [128, TT, H])
        attn = sb("attn", [128, TT, C])
        attnT = sb("attnT", [128, S])
        squares = sb("squares", [128, TT, C], BF16)
        sums = sb("sums", [128, 2, TT])
        mean_var = sb("mean_var", [128, TT, 2])
        stats = sb("stats", [128, TT, 6])
        var_eps = sb("var_eps", [128, TT])
        rstd = sb("rstd", [128, TT])
        rms = sb("rms", [128, 2, TT])
        rms_in = sb("rms_in", [128, TT])
        x1T = sb("x1T", [128, S])
        hidden = sb("hidden", [128, 4, S])
        prod = sb("prod", [128, 2, 2, EPG, C])
        logit = sb("logit", [128, TT, E_GRP + E])
        g_diff = sb("g_diff", [128, TT, 1])
        second = sb("second", [128, TT, 1])
        first = sb("first", [128, TT, 1])
        g_sign = sb("g_sign", [128, TT, 1])
        e_in = sb("e_in", [128, TT, EPG])
        e_tmp = sb("e_tmp", [128, TT, EPG])
        e_max = sb("e_max", [128, TT, 1])
        z = sb("z", [128, TT, EPG + 1])
        ez = sb("ez", [128, TT, EPG + 1])
        e_sum = sb("e_sum", [128, TT, 1])
        g_den = sb("g_den", [128, TT, 1])
        e_den = sb("e_den", [128, TT, 1])
        e_rden = sb("e_rden", [128, TT, 1])
        beaten = sb("beaten", [128, TT, EPG])
        above = sb("above", [128, TT, EPG])
        e_w = sb("e_w", [128, TT, EPG])
        gate = sb("gate", [128, TT, E])
        wq = sb("wq", [128, C])
        wk = sb("wk", [128, C])
        wv = sb("wv", [128, C])
        wo = sb("wo", [128, C])
        kcT = probs[0:DC, 0, 0, 0:2 * C].rearrange("p (i c) -> p i c", i=2)
        kv2 = probs[0:DC, 0, 1, 0:2 * C].rearrange("p (i c) -> p i c", i=2)
        awq = sb("awq", [C // 2, 3, C // 2])
        awo = sb("awo", [C // 2, C])
        w_in = sb("w_in", [128, 2, 2 * HID])
        w_out = sb("w_out", [128, 2, C])
        w2 = sb("w2", [128, 2, E, C])
        w_gate = sb("w_gate", [128, E_GRP + E])
        b_gate = sb("b_gate", [128, 1, E_GRP + E])
        bo = sb("bo", [128, 1, C])
        n1 = sb("n1", [128, C])
        n2 = sb("n2", [128, C])
        cosT = sb("cosT", [128, S])
        sinT = sb("sinT", [128, S])
        ident = sb("ident", [128, 128])
        identb = sb("identb", [128, 128], BF16)
        power = sb("power", [128, TT])
        ones_row = sb("ones_row", [PARTS, 1, S], BF16)
        order0 = sb("order0", [128, TT, EPG])

        ps_max = ctx.enter_context(nc.psum_tensor("ps_max", [128, MAX_RING, S], F32))
        ps_exp = ctx.enter_context(nc.psum_tensor("ps_exp", [128, EXP_RING, S], F32))
        ps_out = ctx.enter_context(nc.psum_tensor("ps_out", [128, S], F32))
        ps = ctx.enter_context(nc.psum_tensor("ps", [128, 2, S], F32))

        scratch = nc.dram_tensor("qk_parts", [2, 2, PARTS, C // H, H, S], BF16, kind="Internal").ap()
        scratch_max = nc.dram_tensor("max_parts_rows", [2, PARTS, HH, S], BF16, kind="Internal").ap()

        early_loaded = sem("early_loaded")
        late_loaded = sem("late_loaded")
        x_loaded = sem("x_loaded")
        fused_done = sem("fused_done")
        fused_copied = sem("fused_copied")
        ones_set = sem("ones_set")
        aug_cleared = sem("aug_cleared")
        tables_loaded = sem("tables_loaded")
        identb_set = sem("identb_set")
        x0_loaded = sem("x0_loaded")
        pool_seq = sem("pool_seq")
        dve_seq = sem("dve_seq")
        spare = [ps[:, i, :] for i in range(2)] + [ps_max[:, i, :] for i in range(MAX_RING)]
        spare += [ps_exp[:, i, :] for i in range(EXP_RING)]
        bank_full = [sem(f"bank_full{i}") for i in range(len(spare))]
        bank_free = [sem(f"bank_free{i}") for i in range(len(spare))]
        stats_done = sem("stats_done")
        rstd_done = sem("rstd_done")
        src_done = sem("src_done")
        part_done = sem("part_done")
        parts_stored = [sem("q_parts_stored"), sem("k_parts_stored")]
        aug_loaded = [sem(f"aug_loaded{i}") for i in range(AUG_RING)]
        max_full = sem("max_full")
        max_done = sem("max_done")
        max_split = sem("max_split")
        maxT_stored = sem("maxT_stored")
        max_loaded = [sem("max_loaded0"), sem("max_loaded1")]
        exp_full = sem("exp_full")
        exp_done = sem("exp_done")
        out_done = sem("out_done")
        heads_done = sem("heads_done")
        sums_done = sem("sums_done")
        rms_done = sem("rms_done")
        x1_done = sem("x1_done")
        router_pool = sem("router_pool")
        router_dve = sem("router_dve")
        router_act = sem("router_act")
        tanh_done = sem("tanh_done")
        expert_added = sem("expert_added")
        norm_done = sem("norm_done")
        x_done = sem("x_done")
        finished = sem("finished")
        stored = sem("stored")

        early = [
            (ident[:, :], w["ident"]), (kcT[:, 0, :], w["ffn_Wk_cT"]), (kv2[:, 0, :], w["ffn_Wk"]),
            (kcT[:, 1, :], w["ffn_Wv_cT"]), (kv2[:, 1, :], w["ffn_Wv"]),
            (wq[:, :], w["ffn_Wq"]),
        ]
        late = [
            (wo[:, :], w["ffn_Wo"]),
            (awq[:, 0, :], w["attn_WqT"]), (awq[:, 1, :], w["attn_WkT"]), (awq[:, 2, :], w["attn_WvT"]),
            (awo[:, :], w["attn_WoT"]),
            (w_in[:, 0, :], w["ffn_W_shared_in"]), (w_in[:, 1, :], w["ffn_W1_shared"]),
            (w_out[:, :, :], w["ffn_W_shared_out"].rearrange("(k p) n -> p k n", p=128)),
            (w2[:, 0, :, :], w["ffn_W2_experts"][:, 0:128, :].rearrange("e p n -> p e n")),
            (w2[:, 1, :, :], w["ffn_W2_experts"][:, 128:256, :].rearrange("e p n -> p e n")),
            (w_gate[:, 0:E_GRP], w["ffn_Wg_gate"]), (w_gate[:, E_GRP:], w["ffn_We_gate"]),
            (b_gate[:, 0, 0:E_GRP], w["ffn_group_bias"].partition_broadcast(128)),
            (b_gate[:, 0, E_GRP:], w["ffn_expert_bias"].partition_broadcast(128)),
            (bo[:, 0, :], w["attn_bo"].partition_broadcast(128)),
            (n1[:, :], w["ffn_norm1_w"].partition_broadcast(128)),
            (n2[:, :], w["ffn_norm2_w"].partition_broadcast(128)),
        ]
        EARLY, LATE = 16 * len(early), 16 * len(late)
        scale = float(np.float32(1) / np.sqrt(np.float32(C // H)))

        uses = {(name, u, *args): use for name, u, args, use in steps}

        def pe_done(engine, *step):
            i, n = uses[step][-1]
            engine.wait_ge(bank_full[i], n + 1)

        def stacked(engine, u):
            engine.wait_ge(aug_loaded[u % AUG_RING], 16 * sum(stack_dmas(v) for v in range(u % AUG_RING, u + 1, AUG_RING)))

        def taken(engine, *step):
            for i, n in uses[step]:
                engine.wait_ge(bank_free[i], n + 1)

        block = ctx.enter_context(nc.Block())

        def experts_added(engine, u):
            if u in VECTOR_EXPERTS:
                for t in range(TT):
                    taken(engine, "expert", u, t, 1)
            else:
                engine.wait_ge(expert_added, TT * (ffn_index(u) + 1))

        def split(eng, seq, own_wait, u, qk):
            rows = H * head_dim(u)
            q = qf[0:rows, :]
            taken(eng, "qk_project", u, qk)
            if is_ffn(u):
                seq(eng.tensor_tensor(rope_s[:, :], rope_s[:, :], sinT[:, :], ALU.mult))
                own_wait()
                if u + qk:
                    eng.wait_ge(part_done, PARTS * (2 * u + qk))
                seq(eng.tensor_tensor(q, rope_c[:, :], rope_s[:, :], ALU.add))
                own_wait()
            if u:
                eng.wait_ge(parts_stored[qk], PARTS * 16 * u)
            h, m, l = (parts[0:rows, qk, c, :] for c in range(PARTS))
            n = PARTS * (2 * u + qk)
            eng.tensor_copy(h, q).then_inc(part_done, 1)
            eng.wait_ge(part_done, n + 1)
            seq(eng.tensor_tensor(rest[0:rows, :], q, h, ALU.subtract))
            own_wait()
            eng.tensor_copy(m, rest[0:rows, :]).then_inc(part_done, 1)
            eng.wait_ge(part_done, n + 2)
            eng.tensor_tensor(l, rest[0:rows, :], m, ALU.subtract).then_inc(part_done, 1)

        @block.sync
        def _(sp):
            sp.dma_start(X[:, 0, :, :], x[0].rearrange("(t p) c -> p t c", p=128)).then_inc(x0_loaded, 16)
            for to, of in early[1::2]:
                sp.dma_start(to, of).then_inc(early_loaded, 16)
            for to, of in ((cosT, w["cosT"]), (sinT, w["sinT"])):
                sp.dma_start(to[:, :], of).then_inc(tables_loaded, 16)
            for b in range(1, B):
                sp.dma_start(X[:, b, :, :], x[b].rearrange("(t p) c -> p t c", p=128)).then_inc(x_loaded, 16)
            for to, of in late:
                sp.dma_start(to, of).then_inc(late_loaded, 16)
            for name, u, args, use in steps:
                d, r, f = head_dim(u), u % AUG_RING, ffn_index(u)
                rows = H * d
                if name == "qk_split":
                    qk, = args
                    if u >= 2 and qk == 0:
                        stacked(sp, u - 2)
                    for c in range(PARTS):
                        sp.wait_ge(part_done, PARTS * (2 * u + qk) + c + 1)
                        sp.dma_start(scratch[u % 2, qk, c, 0:d, :, :].rearrange("d h n -> h d n"),
                                     parts[0:rows, qk, c, :]).then_inc(parts_stored[qk], 16)
                elif name == "stack":
                    qk, = args
                    sp.wait_ge(parts_stored[qk], PARTS * 16 * (u + 1))
                    if u < 2:
                        sp.wait_ge(aug_cleared, u + 1)
                    if u >= AUG_RING:
                        sp.wait_ge(exp_full, TILES * (u - AUG_RING + 1))
                    aug = (q_aug, k_aug)[qk]
                    v = scratch[u % 2, qk, :, 0:d, :, :]
                    for s in range(PARTS):
                        of = v if qk else v[s:s + 1].to_broadcast([PARTS, d, H, S])
                        sp.dma_start(aug[PARTS * d * s:PARTS * d * (s + 1), r, :, :], of).then_inc(aug_loaded[r], 16)
                    if qk:
                        p0 = product_rows(u)
                        sp.dma_start(k_aug[p0:p0 + PARTS, r, :, :], ones_row[:, :, :].to_broadcast([PARTS, H, S]))\
                            .then_inc(aug_loaded[r], 16)
                        if p0 < product_rows(0):
                            n = product_rows(0) - p0
                            sp.dma_start(k_aug[p0 + PARTS:p0 + PARTS + n, r, :, :],
                                         k_aug[128 - n:128, r, :, :]).then_inc(aug_loaded[r], 16)
                elif name == "max_rows":
                    half, = args
                    taken(sp, "max_rows", u, half)
                    if u:
                        sp.wait_ge(max_loaded[half], 16 * u)
                    sp.dma_start(scratch_max[half].rearrange("c h n -> (c h) n"), maxT[:, :]).then_inc(maxT_stored, 16)
                    sp.wait_ge(maxT_stored, 16 * (2 * u + half + 1))
                    p0 = product_rows(u)
                    sp.dma_start(q_aug[p0:p0 + PARTS, r, half * HH:(half + 1) * HH, :],
                                 scratch_max[half]).then_inc(max_loaded[half], 16)
                elif name == "unit_out" and u // B == LAYERS - 1:
                    b = u % B
                    sp.wait_ge(x_done, u + 1)
                    sp.dma_start(out[b].rearrange("(t p) c -> p t c", p=128), X[:, b, :, :]).then_inc(stored, 16)
                elif name == "finish":
                    t, = args
                    sp.wait_ge(finished, t + 1)
                    sp.dma_start(out[u % B, t * 128:(t + 1) * 128, :], X[:, u % B, t, :]).then_inc(stored, 16)
            sp.wait_ge(stored, 16 * (B - 1 + TT))

        @block.tensor
        def _(pe):
            def bank(use):
                i, n = use
                if n:
                    pe.wait_ge(bank_free[i], n)
                elif 2 <= i < 2 + MAX_RING:
                    pe.wait_ge(max_done, UNITS * TILES)
                elif i >= 2:
                    pe.wait_ge(exp_done, UNITS * TILES)
                return spare[i]

            pe.wait_ge(early_loaded, EARLY)
            for i in range(2):
                pe.matmul(ps_out[:, i * C:(i + 1) * C], kcT[:, i, :], kv2[:, i, :], start=True, stop=True).then_inc(fused_done, 1)
            for name, u, args, use in steps:
                d, r, b, f, ffn = head_dim(u), u % AUG_RING, u % B, ffn_index(u), is_ffn(u)
                rows = H * d
                if name == "x_transpose":
                    pe.wait_ge(src_done, u + 1)
                    o = bank(use[0])
                    for t in range(TT):
                        mm = pe.transpose(o[0:rows, t * 128:(t + 1) * 128], src[:, b, t, 0:rows], ident[:, :])
                    mm.then_inc(bank_full[use[0][0]], 1)
                elif name == "qk_project":
                    qk, = args
                    taken(pe, "x_transpose", u)
                    if u == 0 and qk == 0:
                        pe.wait_ge(fused_copied, 1)
                    pe.matmul(bank(use[0])[0:rows, :], (wq, wk)[qk][:, :] if ffn else awq[:, qk, :], xT[0:rows, :],
                              start=True, stop=True).then_inc(bank_full[use[0][0]], 1)
                elif name == "v_project":
                    taken(pe, "x_transpose", u)
                    o = bank(use[0])
                    wv_ = wv[:, :] if ffn else awq[:, 2, :]
                    for t in range(TT):
                        mm = pe.matmul(o[:, t * rows:(t + 1) * rows], xT[0:rows, t * 128:(t + 1) * 128], wv_,
                                       start=True, stop=True)
                    mm.then_inc(bank_full[use[0][0]], 1)
                elif name == "max_scores":
                    h, qt = args
                    n, k = u * TILES + h * TT + qt, product_rows(u)
                    if h == 0 and qt == 0:
                        stacked(pe, u)
                    if n >= MAX_RING:
                        pe.wait_ge(max_done, n - MAX_RING + 1)
                    pe.matmul(ps_max[:, n % MAX_RING, :], q_aug[0:k, r, h, qt * 128:(qt + 1) * 128],
                              k_aug[0:k, r, h, :], start=True, stop=True).then_inc(max_full, 1)
                elif name == "max_rows":
                    half, = args
                    pe.wait_ge(max_split, 2 * u + half + 1)
                    if u + half == 0:
                        pe.wait_ge(identb_set, 1)
                    o = bank(use[0]).bitcast(BF16)
                    for t in range(TT):
                        mm = pe.transpose(o[0:PARTS * HH, t * 128:(t + 1) * 128],
                                          max_parts[:, t, :, :].rearrange("p c h -> p (c h)"), identb[:, :])
                    mm.then_inc(bank_full[use[0][0]], 1)
                elif name == "exp_scores":
                    s, c = args
                    kt, h = s % TT, 4 * (s // TT) + c
                    n = u * TILES + 4 * s + c
                    if h % HH == 0 and kt == 0:
                        pe.wait_ge(max_loaded[h // HH], 16 * (u + 1))
                    if n >= EXP_RING:
                        pe.wait_ge(exp_done, n - EXP_RING + 1)
                    pe.matmul(ps_exp[:, n % EXP_RING, :], k_aug[:, r, h, kt * 128:(kt + 1) * 128],
                              q_aug[:, r, h, :], start=True, stop=True).then_inc(exp_full, 1)
                elif name == "weigh_v":
                    s, = args
                    g, kt, n = s // TT, s % TT, u * 16 + s
                    pe.wait_ge(exp_done, 4 * (n + 1))
                    if s == 0:
                        taken(pe, "v_project", u)
                    if kt == 0 and u * G4 + g:
                        pe.wait_ge(heads_done, u * G4 + g)
                    for c in range(4):
                        h = 4 * g + c
                        mm = pe.matmul(ps_out[COL * c:COL * c + VW, :], v_aug[:, r, kt, h * VW:(h + 1) * VW],
                                       probs[:, n % P_RING, c, :], start=(kt == 0), stop=(kt == TT - 1))
                    mm.then_inc(out_done, 1)
                elif name == "heads_out":
                    t, = args
                    if t == 0:
                        pe.wait_ge(heads_done, G4 * (u + 1))
                    if u == 0 and t == 0:
                        pe.wait_ge(late_loaded, LATE)
                    o = bank(use[0])
                    for g in range(G4):
                        mm = pe.transpose(o[:, g * 128:(g + 1) * 128], heads[:, g, t * 128:(t + 1) * 128], ident[:, :])
                    mm.then_inc(bank_full[use[0][0]], 1)
                elif name == "heads_transpose":
                    taken(pe, "heads_out", u, TT - 1)
                    o = bank(use[0])
                    for t in range(TT):
                        mm = pe.transpose(o[0:rows, t * 128:(t + 1) * 128], attn[:, t, 0:rows], ident[:, :])
                    mm.then_inc(bank_full[use[0][0]], 1)
                elif name == "out_project":
                    taken(pe, "heads_transpose", u)
                    o = bank(use[0])
                    for t in range(TT):
                        mm = pe.matmul(o[:, t * C:(t + 1) * C], attnT[0:rows, t * 128:(t + 1) * 128],
                                       wo[:, :] if ffn else awo[:, :], start=True, stop=True)
                    mm.then_inc(bank_full[use[0][0]], 1)
                elif name == "x1_transpose":
                    pe.wait_ge(x1_done, f + 1)
                    o = bank(use[0])
                    for t in range(TT):
                        mm = pe.transpose(o[:, t * 128:(t + 1) * 128], src[:, b, t, :], ident[:, :])
                    mm.then_inc(bank_full[use[0][0]], 1)
                elif name == "logits":
                    taken(pe, "x1_transpose", u)
                    o, n = bank(use[0]), E_GRP + E
                    for t in range(TT):
                        mm = pe.matmul(o[:, t * n:(t + 1) * n], x1T[:, t * 128:(t + 1) * 128], w_gate[:, :],
                                       start=True, stop=True)
                    mm.then_inc(bank_full[use[0][0]], 1)
                elif name == "mlp_up":
                    c, = args
                    taken(pe, "x1_transpose", u)
                    for i in range(2):
                        c0 = i * HID + (c % 2) * 128
                        pe.matmul(bank(use[i]), w_in[:, c // 2, c0:c0 + 128], x1T[:, :], start=True, stop=True)\
                          .then_inc(bank_full[use[i][0]], 1)
                elif name == "shared_out":
                    taken(pe, "mlp_up", u, 1)
                    o = bank(use[0])
                    for t in range(TT):
                        for k in range(2):
                            mm = pe.matmul(o[:, t * C:(t + 1) * C], hidden[:, k, t * 128:(t + 1) * 128],
                                           w_out[:, k, :], start=(k == 0), stop=(k == 1))
                    mm.then_inc(bank_full[use[0][0]], 1)
                elif name == "expert":
                    t, half = args
                    taken(pe, "mlp_up", u, 3)
                    o = bank(use[0])
                    for k in range(2):
                        mm = pe.matmul(o, hidden[:, 2 + k, t * 128:(t + 1) * 128],
                                       w2[:, k, half * EPG:(half + 1) * EPG, :].rearrange("p e n -> p (e n)"),
                                       start=(k == 0), stop=(k == 1))
                    mm.then_inc(bank_full[use[0][0]], 1)

        @block.vector
        def _(dve):
            own = [0]

            def seq(ins):
                own[0] += 1
                ins.then_inc(dve_seq, 1)

            def own_wait():
                dve.wait_ge(dve_seq, own[0])

            def full(use):
                i, n = use
                dve.wait_ge(bank_full[i], n + 1)
                return spare[i]

            dve.wait_ge(x0_loaded, 16)
            for name, u, args, use in steps:
                d, r, b, f, ffn = head_dim(u), u % AUG_RING, u % B, ffn_index(u), is_ffn(u)
                rows = H * d
                if name == "norm_stats":
                    if u >= B:
                        dve.wait_ge(x_done, u - B + 1)
                    if u == 1:
                        dve.wait_ge(x_loaded, 16 * (B - 1))
                    if u:
                        dve.wait_ge(src_done, u)
                    for t in range(TT):
                        seq(dve.bn_stats(stats[:, t, :], X[:, b, t, :]))
                    own_wait()
                    for t in range(TT):
                        ins = dve.bn_aggr(mean_var[:, t, :], stats[:, t, :])
                        if t < TT - 1:
                            seq(ins)
                    ins.then_inc(stats_done, 1)
                elif name == "norm_apply":
                    dve.wait_ge(rstd_done, u + 1)
                    own_wait()
                    dve.wait_ge(stats_done, u + 1)
                    for t in range(TT):
                        ins = dve.tensor_scalar(src[:, b, t, :], X[:, b, t, :], mean_var[:, t, 0:1], rstd[:, t:t + 1],
                                                ALU.subtract, ALU.mult)
                    ins.then_inc(src_done, 1)
                    if u == 0:
                        dve.wait_ge(fused_done, 2)
                        seq(dve.tensor_copy(wk[:, :], ps_out[:, 0:C]))
                        seq(dve.tensor_copy(wv[:, :], ps_out[:, C:2 * C]))
                        own_wait()
                        dve.memset(ps_out[:, :], 0.0).then_inc(fused_copied, 1)
                elif name == "qk_project" and ffn:
                    qk, = args
                    if u + qk:
                        dve.wait_ge(part_done, PARTS * (2 * u + qk))
                    o = full(use[0])
                    if u + qk == 0:
                        dve.wait_ge(tables_loaded, 16 * 2)
                    dve.tensor_tensor(rope_c[:, :], o, cosT[:, :], ALU.mult)
                    dve.stream_shuffle(rope_s[:, :], o, [i ^ 1 for i in range(32)]).then_inc(bank_free[use[0][0]], 1)
                elif name == "qk_split" and u in VECTOR_SPLITS:
                    split(dve, seq, own_wait, u, *args)
                elif name == "max_scores":
                    h, qt = args
                    n = u * TILES + h * TT + qt
                    if h == 0 and qt == 0 and u >= 2:
                        dve.wait_ge(max_split, 2 * (u - 1))
                    dve.wait_ge(max_full, n + 1)
                    dve.tensor_reduce(maxes[:, u % 2, h // HH, qt, h % HH:h % HH + 1], ps_max[:, n % MAX_RING, :],
                                      AX.X, ALU.max).then_inc(max_done, 1)
                elif name == "heads_out":
                    t, = args
                    if u == 0 and t == 0:
                        dve.wait_ge(late_loaded, LATE)
                        seq(dve.tensor_scalar(n2[:, :], n2[:, :], 0.5, None, ALU.mult))
                    tile = full(use[0]).rearrange("p (h e) -> p h e", e=COL)
                    seq(dve.reciprocal(denom[:, t, :].unsqueeze(2), tile[:, :, ONE_COL:ONE_COL + 1]))
                    own_wait()
                    if u and t == 0:
                        taken(dve, "heads_transpose", u - 1)
                    ins = dve.tensor_tensor(attn[:, t, 0:rows].rearrange("p (h e) -> p h e", e=d), tile[:, :, 0:d],
                                            denom[:, t, :].unsqueeze(2).to_broadcast([128, H, d]), ALU.mult)
                    ins.then_inc(bank_free[use[0][0]], 1)
                elif name == "out_project":
                    o = full(use[0]).rearrange("p (t c) -> p t c", c=C)
                    if ffn:
                        ins = dve.tensor_tensor(src[:, b, :, :], o, src[:, b, :, :], ALU.add)
                        ins.then_inc(bank_free[use[0][0]], 1)
                    else:
                        ins = dve.tensor_tensor(X[:, b, :, :], o, X[:, b, :, :], ALU.add)
                        ins.then_inc(bank_free[use[0][0]], 1)
                elif name == "rms_apply1":
                    dve.wait_ge(rms_done, 2 * f + 1)
                    taken(dve, "out_project", u)
                    for t in range(TT):
                        ins = dve.scalar_tensor_tensor(out=src[:, b, t, :], in0=src[:, b, t, :], scalar=rms[:, 0, t:t + 1],
                                                       in1=n1[:, :], op0=ALU.mult, op1=ALU.mult)
                    ins.then_inc(x1_done, 1)
                elif name == "logits":
                    if f:
                        dve.wait_ge(router_pool, 4 * f)
                    n = E_GRP + E
                    ins = dve.tensor_tensor(logit[:, :, :], full(use[0])[:, 0:TT * n].rearrange("p (t n) -> p t n", n=n),
                                            b_gate[:, :, :].to_broadcast([128, TT, n]), ALU.add)
                    ins.then_inc(bank_free[use[0][0]], 1)
                elif name == "router":
                    k, = args
                    if k == 1:
                        dve.wait_ge(router_pool, 4 * f + 1)
                        dve.tensor_reduce(e_max[:, :, :], e_in[:, :, :], AX.X, ALU.max).then_inc(router_dve, 1)
                    elif k == 4:
                        dve.wait_ge(router_act, f + 1)
                        dve.tensor_reduce(e_sum[:, :, :], ez[:, :, 0:EPG], AX.X, ALU.add).then_inc(router_dve, 1)
                    elif k == 6:
                        dve.wait_ge(router_pool, 4 * f + 3)
                        dve.reciprocal(e_rden[:, :, :], e_den[:, :, :]).then_inc(router_dve, 1)
                elif name == "mlp_up":
                    c, = args
                    dve.wait_ge(tanh_done, 4 * f + c + 1)
                    ins = dve.scalar_tensor_tensor(out=hidden[:, c, :], in0=hidden[:, c, :], scalar=1.0, in1=full(use[0]),
                                                   op0=ALU.add, op1=ALU.mult)
                    ins.then_inc(bank_free[use[0][0]], 1)
                    dve.wait_ge(bank_free[use[0][0]], use[0][1] + 1)
                    ins = dve.scalar_tensor_tensor(out=hidden[:, c, :], in0=hidden[:, c, :], scalar=0.5, in1=full(use[1]),
                                                   op0=ALU.mult, op1=ALU.mult)
                    ins.then_inc(bank_free[use[1][0]], 1)
                elif name == "shared_out":
                    dve.wait_ge(x1_done, f + 1)
                    ins = dve.tensor_tensor(src[:, b, :, :], full(use[0]).rearrange("p (t c) -> p t c", c=C),
                                            src[:, b, :, :], ALU.add)
                    ins.then_inc(bank_free[use[0][0]], 1)
                elif name == "expert":
                    t, half = args
                    dve.wait_ge(router_pool, 4 * (f + 1))
                    o = full(use[0]).rearrange("p (e c) -> p e c", c=C)
                    if u in VECTOR_EXPERTS:
                        if t == half == 0:
                            taken(dve, "shared_out", u)
                        for e in range(EPG):
                            ins = dve.scalar_tensor_tensor(out=src[:, b, t, :], in0=o[:, e, :],
                                                           scalar=gate[:, t, half * EPG + e:half * EPG + e + 1],
                                                           in1=src[:, b, t, :], op0=ALU.mult, op1=ALU.add)
                            if e < EPG - 1:
                                seq(ins)
                                own_wait()
                        ins.then_inc(bank_free[use[0][0]], 1)
                        dve.wait_ge(bank_free[use[0][0]], use[0][1] + 1)
                    else:
                        n = sum(TT for v in range(u) if is_ffn(v)) + t
                        if n >= 2 and half == 0:
                            dve.wait_ge(expert_added, n - 1)
                        dve.tensor_tensor(prod[:, n % 2, half, :, :], o,
                                          gate[:, t, half * EPG:(half + 1) * EPG].unsqueeze(2)
                                          .to_broadcast([128, EPG, C]), ALU.mult).then_inc(bank_free[use[0][0]], 1)
                elif name == "rms_apply2":
                    dve.wait_ge(rms_done, 2 * f + 2)
                    experts_added(dve, u)
                    for t in range(TT):
                        ins = dve.scalar_tensor_tensor(out=src[:, b, t, :], in0=src[:, b, t, :],
                                                       scalar=rms[:, 1, t:t + 1], in1=n2[:, :],
                                                       op0=ALU.mult, op1=ALU.mult)
                    ins.then_inc(norm_done, 1)

                elif name == "finish":
                    t, = args
                    dve.wait_ge(rms_done, 2 * f + 2 + t)
                    seq(dve.scalar_tensor_tensor(out=src[:, b, t, :], in0=src[:, b, t, :], scalar=rms[:, 1, t:t + 1],
                                                 in1=n2[:, :], op0=ALU.mult, op1=ALU.mult))
                    own_wait()
                    dve.tensor_tensor(X[:, b, t, :], X[:, b, t, :], src[:, b, t, :], ALU.add).then_inc(finished, 1)

        @block.scalar
        def _(act):
            def full(use):
                i, n = use
                act.wait_ge(bank_full[i], n + 1)
                return spare[i]

            for to, of in early[0::2]:
                act.dma_start(to, of).then_inc(early_loaded, 16)
            act.wait_ge(early_loaded, EARLY)
            act.activation(identb[:, :], ident[:, :], ACT.Copy).then_inc(identb_set, 1)
            act.wait_ge(ones_set, 1)
            for name, u, args, use in steps:
                d, r, b, f, ffn = head_dim(u), u % AUG_RING, u % B, ffn_index(u), is_ffn(u)
                rows = H * d
                if name == "x_transpose":
                    if u:
                        pe_done(act, "v_project", u - 1)
                    ins = act.activation(xT[0:rows, :], full(use[0])[0:rows, :], ACT.Copy)
                    ins.then_inc(bank_free[use[0][0]], 1)
                elif name == "qk_project" and not ffn:
                    qk, = args
                    act.wait_ge(part_done, PARTS * (2 * u + qk))
                    ins = act.activation(qf[0:rows, :], full(use[0])[0:rows, :], ACT.Copy)
                    ins.then_inc(bank_free[use[0][0]], 1)
                elif name == "v_project":
                    if u >= AUG_RING:
                        act.wait_ge(out_done, 16 * (u - AUG_RING + 1))
                    to = v_aug[:, r, :, :].rearrange("p t (h e) -> p (t h) e", e=VW)[:, :, 0:d]
                    ins = act.activation(to, full(use[0])[:, 0:TT * rows].rearrange("p (m e) -> p m e", e=d), ACT.Copy)
                    ins.then_inc(bank_free[use[0][0]], 1)
                elif name == "max_rows":
                    half, = args
                    if u + half:
                        act.wait_ge(maxT_stored, 16 * (2 * u + half))
                    n = PARTS * HH
                    ins = act.activation(maxT[:, :], full(use[0]).bitcast(BF16)[0:n, 0:S], ACT.Copy)
                    ins.then_inc(bank_free[use[0][0]], 1)
                elif name == "exp_scores":
                    s, c = args
                    n, step = u * TILES + 4 * s + c, u * 16 + s
                    act.wait_ge(exp_full, n + 1)
                    if c == 0 and step >= P_RING:
                        act.wait_ge(out_done, step - P_RING + 1)
                    act.activation(probs[:, step % P_RING, c, :], ps_exp[:, n % EXP_RING, :], ACT.Exp,
                                   scale=scale).then_inc(exp_done, 1)
                elif name == "heads_evacuate":
                    g, = args
                    act.wait_ge(out_done, u * 16 + TT * (g + 1))
                    if u:
                        pe_done(act, "heads_out", u - 1, TT - 1)
                    act.activation(heads[:, g, :], ps_out[:, :], ACT.Copy).then_inc(heads_done, 1)
                elif name == "heads_transpose":
                    if u:
                        pe_done(act, "out_project", u - 1)
                    ins = act.activation(attnT[0:rows, :], full(use[0])[0:rows, :], ACT.Copy)
                    ins.then_inc(bank_free[use[0][0]], 1)
                elif name == "rms_stats":
                    which, = args
                    if which == 0:
                        taken(act, "out_project", u)
                    else:
                        experts_added(act, u)
                    if f + which:
                        act.wait_ge(sums_done, 2 * f + which)
                    if f:
                        act.wait_ge(rms_done, 2 * f - 1 + which)
                    for t in range(TT):
                        ins = act.activation(squares[:, t, :], src[:, b, t, :], ACT.Square, accum_out=sums[:, which, t:t + 1])
                    ins.then_inc(sums_done, 1)
                elif name == "finish":
                    t, = args
                    taken(act, "expert", u, t, 1)
                    act.wait_ge(rms_done, 2 * f + 1)
                    act.activation(squares[:, t, :], src[:, b, t, :], ACT.Square,
                                   accum_out=sums[:, 1, t:t + 1]).then_inc(sums_done, 1)
                elif name == "x1_transpose":
                    if f:
                        pe_done(act, "mlp_up", before(u), 3)
                    ins = act.activation(x1T[:, :], full(use[0]), ACT.Copy)
                    ins.then_inc(bank_free[use[0][0]], 1)
                elif name == "router" and args[0] == 3:
                    act.wait_ge(router_pool, 4 * f + 2)
                    act.activation(ez[:, :, :], z[:, :, :], ACT.Exp).then_inc(router_act, 1)
                elif name == "mlp_up":
                    c, = args
                    if f:
                        pe_done(act, *(("shared_out", before(u)) if c < 2 else ("expert", before(u), TT - 1, 1)))
                    act.activation(hidden[:, c, :], full(use[0]), ACT.Tanh, scale=0.5).then_inc(tanh_done, 1)

        @block.gpsimd
        def _(pool):
            own = [0]

            def seq(ins):
                own[0] += 1
                ins.then_inc(pool_seq, 1)
                return ins

            def own_wait():
                pool.wait_ge(pool_seq, own[0])

            seq(pool.memset(v_aug[:, :, :, :], 0.0))
            own_wait()
            seq(pool.memset(power[:, :], -0.5))
            seq(pool.memset(ones_row[:, :, :], 1.0))
            for e in range(EPG):
                seq(pool.memset(order0[:, :, e:e + 1], float(e)))
            own_wait()
            ones = v_aug[:, :, :, :].rearrange("p r t (h e) -> p (r t h) e", e=VW)[:, :, ONE_COL:ONE_COL + 1]
            pool.memset(ones, 1.0).then_inc(ones_set, 1)
            pool.wait_ge(ones_set, 1)
            for name, u, args, use in steps:
                d, r, b, f, ffn = head_dim(u), u % AUG_RING, u % B, ffn_index(u), is_ffn(u)
                rows = H * d
                if name == "norm_stats":
                    pool.wait_ge(stats_done, u + 1)
                    seq(pool.tensor_scalar(var_eps[:, :].unsqueeze(2), mean_var[:, :, 1:2], LN_EPS, None, ALU.add))
                    own_wait()
                    if u:
                        pool.wait_ge(src_done, u)
                    pool.tensor_tensor(rstd[:, :], var_eps[:, :], power[:, :], ALU.pow).then_inc(rstd_done, 1)
                    if u < 2:
                        pool.wait_ge(rstd_done, u + 1)
                        if u == 0:
                            seq(pool.memset(k_aug[64:128, 0:1, :, :].bitcast(F32), 0.0))
                            own_wait()
                            pool.memset(q_aug[64:128, 0:1, :, :].bitcast(F32), 0.0).then_inc(aug_cleared, 1)
                            pool.wait_ge(aug_cleared, 1)
                            seq(pool.memset(k_aug[64:128, 1:, :, :].bitcast(F32), 0.0))
                            own_wait()
                        else:
                            pool.memset(q_aug[64:128, 1:, :, :].bitcast(F32), 0.0).then_inc(aug_cleared, 1)
                            pool.wait_ge(aug_cleared, 2)
                elif name == "qk_split" and u not in VECTOR_SPLITS:
                    split(pool, seq, own_wait, u, *args)
                elif name == "max_parts":
                    half, = args
                    pool.wait_ge(max_done, u * TILES + TILES // 2 * (half + 1))
                    if u + half:
                        pe_done(pool, "max_rows", *((u, 0) if half else (u - 1, 1)))
                    mx = maxes[:, u % 2, half, :, :]
                    h, m, l = (max_parts[:, :, c, :] for c in range(PARTS))
                    seq(pool.tensor_scalar(h, mx, -1.0, None, ALU.mult))
                    own_wait()
                    seq(pool.tensor_tensor(max_rest[:, :, :], mx, h, ALU.add))
                    own_wait()
                    seq(pool.tensor_scalar(m, max_rest[:, :, :], -1.0, None, ALU.mult))
                    own_wait()
                    seq(pool.tensor_tensor(max_rest[:, :, :], max_rest[:, :, :], m, ALU.add))
                    own_wait()
                    pool.tensor_scalar(l, max_rest[:, :, :], -1.0, None, ALU.mult).then_inc(max_split, 1)
                elif name == "rms_stats":
                    which, = args
                    pool.wait_ge(sums_done, 2 * f + which + 1)
                    seq(pool.tensor_scalar(rms_in[:, :], sums[:, which, :], 1.0 / C, RMS_EPS, ALU.mult, ALU.add))
                    own_wait()
                    if f:
                        pool.wait_ge((x1_done, norm_done)[which], f)
                    pool.tensor_tensor(rms[:, which, :], rms_in[:, :], power[:, :], ALU.pow).then_inc(rms_done, 1)
                elif name == "router":
                    k, = args
                    wide = [128, TT, EPG]
                    if k == 0:
                        taken(pool, "logits", u)
                        if f:
                            pool.wait_ge(router_dve, 3 * f)
                        seq(pool.tensor_tensor(g_diff[:, :, :], logit[:, :, 1:2], logit[:, :, 0:1], ALU.subtract))
                        own_wait()
                        seq(pool.tensor_scalar(second[:, :, :], g_diff[:, :, :], 0.0, None, ALU.is_gt))
                        own_wait()
                        seq(pool.tensor_scalar(first[:, :, :], second[:, :, :], -1.0, 1.0, ALU.mult, ALU.add))
                        seq(pool.tensor_tensor(e_tmp[:, :, :], logit[:, :, E_GRP + EPG:], second[:, :, :].to_broadcast(wide),
                                               ALU.mult))
                        own_wait()
                        seq(pool.tensor_tensor(e_in[:, :, :], logit[:, :, E_GRP:E_GRP + EPG],
                                               first[:, :, :].to_broadcast(wide), ALU.mult))
                        own_wait()
                        pool.tensor_tensor(e_in[:, :, :], e_in[:, :, :], e_tmp[:, :, :], ALU.add).then_inc(router_pool, 1)
                    elif k == 2:
                        pool.wait_ge(router_dve, 3 * f + 1)
                        seq(pool.tensor_tensor(z[:, :, 0:EPG], e_in[:, :, :], e_max[:, :, :].to_broadcast(wide),
                                               ALU.subtract))
                        seq(pool.tensor_tensor(g_sign[:, :, :], first[:, :, :], second[:, :, :], ALU.subtract))
                        own_wait()
                        pool.tensor_tensor(z[:, :, EPG:EPG + 1], g_diff[:, :, :], g_sign[:, :, :], ALU.mult)\
                            .then_inc(router_pool, 1)
                        seq(pool.tensor_copy(beaten[:, :, :], order0[:, :, :]))
                        for s in range(1, EPG):
                            lo, hi, n = slice(0, EPG - s), slice(s, EPG), EPG - s
                            seq(pool.tensor_tensor(above[:, :, 0:n], e_in[:, :, hi], e_in[:, :, lo], ALU.subtract))
                            own_wait()
                            seq(pool.tensor_scalar(above[:, :, 0:n], above[:, :, 0:n], 0.0, None, ALU.is_gt))
                            own_wait()
                            seq(pool.tensor_tensor(beaten[:, :, lo], beaten[:, :, lo], above[:, :, 0:n], ALU.add))
                            own_wait()
                            seq(pool.tensor_tensor(beaten[:, :, hi], beaten[:, :, hi], above[:, :, 0:n], ALU.subtract))
                            own_wait()
                        seq(pool.tensor_scalar(beaten[:, :, :], beaten[:, :, :], 1.5, None, ALU.is_lt))
                    elif k == 5:
                        pool.wait_ge(router_dve, 3 * f + 2)
                        seq(pool.tensor_scalar(g_den[:, :, :], ez[:, :, EPG:EPG + 1], 1.0, None, ALU.add))
                        own_wait()
                        pool.tensor_tensor(e_den[:, :, :], e_sum[:, :, :], g_den[:, :, :], ALU.mult)\
                            .then_inc(router_pool, 1)
                        seq(pool.tensor_tensor(e_w[:, :, :], ez[:, :, 0:EPG], beaten[:, :, :], ALU.mult))
                    elif k == 7:
                        pool.wait_ge(router_dve, 3 * f + 3)
                        own_wait()
                        seq(pool.tensor_tensor(e_w[:, :, :], e_w[:, :, :], e_rden[:, :, :].to_broadcast(wide), ALU.mult))
                        own_wait()
                        if f:
                            taken(pool, "expert", before(u), TT - 1, 1)
                        seq(pool.tensor_tensor(gate[:, :, 0:EPG], e_w[:, :, :], first[:, :, :].to_broadcast(wide), ALU.mult))
                        own_wait()
                        pool.tensor_tensor(gate[:, :, EPG:], e_w[:, :, :], second[:, :, :].to_broadcast(wide), ALU.mult)\
                            .then_inc(router_pool, 1)
                elif name == "expert" and args[1] == 1 and u not in VECTOR_EXPERTS:
                    t = args[0]
                    taken(pool, "expert", u, t, 0)
                    taken(pool, "expert", u, t, 1)
                    if t == 0:
                        taken(pool, "shared_out", u)
                    p = prod[:, (f * TT + t) % 2, :, :, :]
                    seq(pool.tensor_tensor(p[:, 0, :, :], p[:, 0, :, :], p[:, 1, :, :], ALU.add))
                    own_wait()
                    seq(pool.tensor_tensor(p[:, 0, 0:2, :], p[:, 0, 0:2, :], p[:, 0, 2:4, :], ALU.add))
                    own_wait()
                    seq(pool.tensor_tensor(src[:, b, t, :], src[:, b, t, :], p[:, 0, 0, :], ALU.add))
                    own_wait()
                    pool.tensor_tensor(src[:, b, t, :], src[:, b, t, :], p[:, 0, 1, :], ALU.add).then_inc(expert_added, 1)
                elif name == "finish":
                    t, = args
                    pool.wait_ge(sums_done, 2 * f + 2 + t)
                    seq(pool.tensor_scalar(rms_in[:, t:t + 1], sums[:, 1, t:t + 1], 1.0 / C, RMS_EPS, ALU.mult, ALU.add))
                    own_wait()
                    if t == 0:
                        pool.wait_ge(norm_done, f)
                    pool.tensor_tensor(rms[:, 1, t:t + 1], rms_in[:, t:t + 1], power[:, t:t + 1], ALU.pow)\
                        .then_inc(rms_done, 1)
                elif name == "unit_out":
                    if ffn:
                        pool.wait_ge(norm_done, f + 1)
                        if u >= B:
                            pool.wait_ge(x_done, u - B + 1)
                        pool.tensor_tensor(X[:, b, :, :], X[:, b, :, :], src[:, b, :, :], ALU.add).then_inc(x_done, 1)
                    else:
                        taken(pool, "out_project", u)
                        if u == B:
                            pool.wait_ge(late_loaded, LATE)
                        pool.tensor_tensor(X[:, b, :, :], X[:, b, :, :], bo[:, :, :].to_broadcast([128, TT, C]), ALU.add)\
                            .then_inc(x_done, 1)


_PLAIN = ["ffn_Wq", "ffn_Wo", "ffn_Wk", "ffn_Wv", "ffn_W_shared_in", "ffn_W1_shared", "ffn_W_shared_out",
          "ffn_W2_experts", "ffn_Wg_gate", "ffn_We_gate", "ffn_group_bias", "ffn_expert_bias", "ffn_norm1_w",
          "ffn_norm2_w", "attn_bo"]
_TURNED = ["ffn_Wk_c", "ffn_Wv_c", "attn_Wq", "attn_Wk", "attn_Wv", "attn_Wo"]


def shape_constants():
    dh = C // H
    inv = (1.0 / np.power(np.float32(10000.0), np.arange(0, dh, 2, dtype=np.float32) / np.float32(dh))).astype(np.float32)
    ang = np.arange(S, dtype=np.float32)[:, None] * inv[None, :]
    rows = (np.arange(C) % dh) // 2
    sign = np.where(np.arange(C) % 2 == 0, np.float32(-1), np.float32(1))[:, None]
    out = {"cosT": np.cos(ang).T[rows], "sinT": sign * np.sin(ang).T[rows], "ident": np.eye(128)}
    out = {k: np.ascontiguousarray(v, dtype=np.float32) for k, v in out.items()}
    return out


def kernel(**inputs):
    import concourse.bacc as _bacc
    from concourse.bass_utils import run_bass_kernel_spmd as _run

    nc = _bacc.Bacc("TRN2", target_bir_lowering=False, num_devices=1)
    arrays = {"x": np.ascontiguousarray(inputs["L0_attn_x"])}
    for name in _PLAIN:
        arrays[name] = np.ascontiguousarray(inputs["L0_" + name])
    for name in _TURNED:
        arrays[name + "T"] = np.ascontiguousarray(np.transpose(inputs["L0_" + name]))
    arrays.update(shape_constants())
    aps, feed = {}, {}
    for name, a in arrays.items():
        feed[f"in_{name}_dram"] = a
        aps[name] = nc.dram_tensor(f"in_{name}_dram", a.shape, mybir.dt.from_np(a.dtype), kind="ExternalInput").ap()
    out = nc.dram_tensor("out_0_dram", (B, S, C), F32, kind="ExternalOutput").ap()
    macaron(nc, aps.pop("x"), aps, out)
    r = _run(nc, [feed], core_ids=[0])
    return r.results[0]["out_0_dram"]
```
